# Optimizing a Trainium2 kernel written in Bass

```python
import numpy as np
import jax
import jax.numpy as jnp

def _softmax(x, axis=-1):
    return jax.nn.softmax(x, axis=axis)

def _gelu(x):
    return jax.nn.gelu(x, approximate=True)

def _silu(x):
    return jax.nn.silu(x)

def _sigmoid(x):
    return jax.nn.sigmoid(x)

def _layernorm(x, axis=-1, eps=1e-05):
    m = jnp.mean(x, axis=axis, keepdims=True)
    v = jnp.var(x, axis=axis, keepdims=True)
    return (x - m) / jnp.sqrt(v + eps)

def _scatter_add(tgt, idx, src, axis=0):
    return tgt.at[idx].add(src)

def _segment_sum(src, seg, n):
    return jax.ops.segment_sum(src, seg, n)
kernel_name = 'mk_gnn_resnorm_d1_gnn_r8_74b01e'

def setup_inputs(seed: int=0):
    np.random.seed(seed)
    _w = jnp.asarray

    def _rec_inputs():
        import jax
        import jax.numpy as jnp
        _gk = jax.random.key(seed)
        x = -8.776e-05 + 1 * jax.random.normal(jax.random.fold_in(_gk, 1), (6250, 256), jnp.float32)
        src = jax.random.randint(jax.random.fold_in(_gk, 2), (100000,), 0, 6250, jnp.int32)
        dst = jax.random.randint(jax.random.fold_in(_gk, 3), (100000,), 0, 6250, jnp.int32)
        _o = jnp.argsort(dst, stable=True)
        src = src[_o]
        dst = dst[_o]
        edge_type_16 = jax.random.randint(jax.random.fold_in(_gk, 12), (100000,), 0, 16, jnp.int32)
        edge_weight1 = jax.random.uniform(jax.random.fold_in(_gk, 13), (100000, 1), jnp.float32, 0.0, 0.999998)
        return (x, src, dst, edge_type_16, edge_weight1)
    x, src, dst, edge_type_16, edge_weight1 = _rec_inputs()

    def _L0_gnn_setup():
        import jax, jax.numpy as jnp
        import numpy as np
        N_NODES = 2500
        N_EDGES = 40000
        NUM_RELS = 16
        IN_FEAT = 256
        OUT_FEAT = 256
        key = jax.random.key(seed)
        k_h, k_w, k_n, k_s, k_d, k_r = jax.random.split(key, 6)
        h = jax.random.normal(k_h, (N_NODES, IN_FEAT), dtype=jnp.float32)
        weight = jax.random.normal(k_w, (NUM_RELS, IN_FEAT, OUT_FEAT), dtype=jnp.float32)
        norm = jax.random.uniform(k_n, (N_EDGES, 1), dtype=jnp.float32)
        src = jax.random.randint(k_s, (N_EDGES,), 0, N_NODES, dtype=jnp.int32)
        dst = jax.random.randint(k_d, (N_EDGES,), 0, N_NODES, dtype=jnp.int32)
        rel_type = jax.random.randint(k_r, (N_EDGES,), 0, NUM_RELS, dtype=jnp.int32)
        return {'h': h, 'weight': weight, 'norm': norm, 'src': src, 'dst': dst, 'rel_type': rel_type}
    _L0_gnn_all = _L0_gnn_setup()
    _L0_gnn_in = {k: v for k, v in _L0_gnn_all.items() if k in ('weight',)}
    del _L0_gnn_all
    return {'x': x, 'src': src, 'dst': dst, 'edge_type_16': edge_type_16, 'edge_weight1': edge_weight1, 'L0_gnn_weight': _L0_gnn_in['weight']}

def reference(x, src, dst, edge_type_16, edge_weight1, L0_gnn_weight):
    import jax
    import jax.numpy as jnp

    def _L0_gnn_ref(h, weight, norm, src, dst, rel_type):
        import jax, jax.numpy as jnp
        import numpy as np
        N_NODES = 2500
        N_EDGES = 40000
        NUM_RELS = 16
        IN_FEAT = 256
        OUT_FEAT = 256
        transformed = jnp.einsum('ni,rio->rno', h, weight)
        msg = transformed[rel_type, src] * norm
        out = jax.ops.segment_sum(msg, dst, num_segments=h.shape[0])
        return out
    x = _layernorm(x + _L0_gnn_ref(x, L0_gnn_weight, edge_weight1, src, dst, edge_type_16), axis=-1)
    return x

_drawn_inputs = setup_inputs


def setup_inputs(seed=0):
    import zlib

    import numpy as np

    out = dict(_drawn_inputs(seed))
    spreads = {}
    factors = {}
    for name, (base, spread) in spreads.items():
        noise = np.random.default_rng([zlib.crc32(name.encode()), seed]).standard_normal(out[name].shape)
        drawn = base * np.exp(spread * noise) if base else spread * noise
        out[name] = jnp.asarray(drawn.astype(out[name].dtype))
    for name, factor in factors.items():
        out[name] = (out[name] * factor).astype(out[name].dtype)
    return out
```

```python
import concourse.bass as bass
from concourse import mybir
from contextlib import ExitStack


P = 128
EPS = 1e-5


def resnorm_gnn(nc, x_rows, x_cols, weight, src_lanes, rel_lanes, dst_lanes, norm_lanes,
                dst_groups, out):
    f32, f32r, i32 = mybir.dt.float32, mybir.dt.float32r, mybir.dt.int32
    ALU, ACT, AX = mybir.AluOpType, mybir.ActivationFunctionType, mybir.AxisListType

    NODES, F = out.shape
    RELS = 2 * weight.shape[0]
    TILES = x_rows.shape[0] // P
    HALVES = F // P
    PAIRS = RELS // 2
    CHUNKS = src_lanes.shape[1]
    GROUP = 8
    HALF_GROUP = GROUP // 2
    GROUPS = CHUNKS // GROUP
    SLOTS = 2 * GROUP
    ROW = RELS * F
    LAST = NODES - (TILES - 1) * P
    assert TILES % 2 == 1 and GROUPS % 2 == 0

    table = nc.dram_tensor("table", [TILES * P * RELS, F], f32).ap()
    range_dram = nc.dram_tensor("range_dram", [GROUPS, 2], i32).ap()
    table_tiles = table.rearrange("(t p r) f -> t p (r f)", p=P, r=RELS)
    xc = x_cols.rearrange("(h p) n -> p h n", p=P)

    ctx = ExitStack()
    with ctx:
        def sb(name, shape, dt):
            return ctx.enter_context(nc.sbuf_tensor(name, shape, dt))

        def sem(name):
            return ctx.enter_context(nc.semaphore(name))

        stage = sb("stage", [P, 2, ROW], f32)
        w_raw = stage[:, :, :].rearrange("p a (k h n) -> p (a k) h n", h=HALVES, n=2 * F)
        rows = stage[:, :, :].rearrange("p a (s f) -> p (a s) f", f=F)
        w_split = sb("w_split", [P, 2, PAIRS, HALVES, 2 * F], f32r)
        msg = w_split[:, :, :, :, :].rearrange("p a k h (two f) -> p a (k h two) f", two=2)
        onehot = sb("onehot", [P, GROUP, P], f32r)
        x_raw = sb("x_raw", [P, 2, HALVES, P], f32)
        x_split = sb("x_split", [P, 2, 2, HALVES, P], f32r)
        acc = sb("acc", [P, TILES, F], f32)
        src_sb = sb("src_sb", [P, CHUNKS], i32)
        rel_sb = sb("rel_sb", [P, CHUNKS], i32)
        row_sb = sb("row_sb", [P, CHUNKS], i32)
        dst_sb = sb("dst_sb", [P, CHUNKS], i32)
        dst_f = sb("dst_f", [P, CHUNKS], f32)
        norm_sb = sb("norm_sb", [P, CHUNKS], f32)
        dst_rel = sb("dst_rel", [P, GROUP], f32)
        row_now = sb("row_now", [P, SLOTS], i32)
        lane = sb("lane", [P, P], f32)
        tile_base = sb("tile_base", [P, TILES], f32)
        dst_g = sb("dst_g", [GROUPS, GROUP * P], i32)
        span = sb("span", [GROUPS, 2], i32)
        span_tile = sb("span_tile", [GROUPS, 2], i32)
        ranges = sb("ranges", [1, 2 * GROUPS], i32)
        stats = sb("stats", [P, TILES, 6], f32)
        mean_var = sb("mean_var", [P, TILES, 2], f32)
        std = sb("std", [P, TILES], f32)
        rstd = sb("rstd", [P, TILES], f32)
        shift = sb("shift", [P, TILES], f32)
        eps = sb("eps", [P, 1], f32)

        bank = [ctx.enter_context(nc.psum_tensor(f"bank{k}", [P, 2 * F], f32)) for k in range(PAIRS)]

        w_in = [sem(f"w_in{k}") for k in range(PAIRS)]
        x_in = [sem("x_in0"), sem("x_in1")]
        w_hi_done, w_lo_done = sem("w_hi_done"), sem("w_lo_done")
        x_hi_done, x_lo_done = sem("x_hi_done"), sem("x_lo_done")
        bank_done = sem("bank_done")
        evac_act, evac_dve = sem("evac_act"), sem("evac_dve")
        stored = [sem("stored0"), sem("stored1")]
        edges_in, acc_in = sem("edges_in"), sem("acc_in")
        consts, span_done, span_out, ranges_in = sem("consts"), sem("span_done"), sem("span_out"), sem("ranges_in")
        rows_named, row_now_done = sem("rows_named"), sem("row_now_done")
        gathered = [sem(f"gathered{s}") for s in range(SLOTS)]
        pool_passed = sem("pool_passed")
        hi_done, lo_done = sem("hi_done"), sem("lo_done")
        dst_rel_done = sem("dst_rel_done")
        onehot_first, onehot_more = sem("onehot_first"), sem("onehot_more")
        sum_first, sum_more = sem("sum_first"), sem("sum_more")
        acc_done, stats_done, std_done, rstd_done = sem("acc_done"), sem("stats_done"), sem("std_done"), sem("rstd_done")
        norm_dve, norm_act = sem("norm_dve"), sem("norm_act")
        out_done = sem("out_done")

        block = ctx.enter_context(nc.Block())

        def col(t, i, n=1):
            return t[:, bass.ds(i, n)]


        @block.sync
        def _(sp):
            def load_x(n, b):
                sp.dma_start(x_raw[:, b], xc[:, :, bass.ds(n * P, P)]).then_inc(x_in[b], 16)

            def store(n, b):
                sp.wait_ge(evac_act, (PAIRS // 2) * (n + 1))
                sp.wait_ge(evac_dve, (PAIRS // 2) * (n + 1))
                sp.dma_start(table_tiles[bass.ds(n, 1)].rearrange("a p n -> (a p) n"),
                             stage[:, b]).then_inc(stored[b], 16)

            load_x(0, 0)
            for k in range(PAIRS):
                sp.dma_start(w_raw[:, k].rearrange("p h n -> p (h n)"), weight[k]).then_inc(w_in[k], 16)
                if k == 0:
                    load_x(1, 1)
            sp.dma_start(acc[:, :, :], x_rows.rearrange("(t p) f -> p t f", p=P)).then_inc(acc_in, 16)
            sp.wait_ge(x_lo_done, 1)
            load_x(2, 0)
            store(0, 0)
            with sp.Fori(0, TILES // 2 - 1) as i:
                for b in (1, 0):
                    n = 2 * i + 2 - b
                    sp.wait_ge(x_lo_done, n + 1)
                    load_x(n + 2, b)
                    store(n, b)
            for n, b in ((TILES - 2, 1), (TILES - 1, 0)):
                store(n, b)
            sp.wait_ge(span_done, 4)
            sp.dma_start(range_dram[:, :], span_tile[:, :]).then_inc(span_out, 16)
            sp.wait_ge(span_out, 16)
            sp.dma_start(ranges[:, :], range_dram.rearrange("g two -> (g two)").rearrange("(a n) -> a n", a=1)).then_inc(ranges_in, 16)
            BATCH = 8
            for t0 in range(0, TILES - 1, BATCH):
                t1 = t0 + BATCH
                sp.wait_ge(norm_dve, (t1 + 1) // 2)
                sp.wait_ge(norm_act, t1 // 2)
                sp.dma_start(out[t0 * P:t1 * P, :].rearrange("(t p) f -> p t f", p=P),
                             acc[:, t0:t1, :]).then_inc(out_done, 16)
            sp.wait_ge(norm_dve, TILES // 2 + 1)
            sp.dma_start(out[(TILES - 1) * P:NODES, :], acc[0:LAST, TILES - 1, :]).then_inc(out_done, 16)
            sp.wait_ge(out_done, 16 * ((TILES - 1) // BATCH + 1))

        @block.gpsimd
        def _(pool):
            pool.iota(lane[:, :], pattern=[[1, P]], base=0, channel_multiplier=0,
                      allow_small_or_imprecise_dtypes=True).then_inc(consts, 1)
            pool.iota(tile_base[:, :], pattern=[[P, TILES]], base=0, channel_multiplier=0,
                      allow_small_or_imprecise_dtypes=True).then_inc(consts, 1)
            pool.memset(eps[:, :], EPS).then_inc(consts, 1)

            def gather(g, b, first):
                pool.wait_ge(row_now_done, g + 1)
                pool.sem_inc(pool_passed, 1)
                for j in range(GROUP):
                    s = b * GROUP + j
                    if not first and j % HALF_GROUP == 0:
                        pool.wait_ge(lo_done, GROUP * (g - 2) + j + HALF_GROUP)
                        pool.sem_inc(pool_passed, 1)
                    pool.indirect_dma_start(
                        out=rows[:, s, :], out_offset=None, in_=table[:, :],
                        in_offset=bass.IndirectOffsetOnAxis(ap=row_now[:, s:s + 1], axis=0),
                    ).then_inc(gathered[s], 16)

            pool.wait_ge(stored[0], 16 * (TILES // 2 + 1))
            pool.wait_ge(stored[1], 16 * (TILES // 2))
            gather(0, 0, True)
            gather(1, 1, True)
            with pool.Fori(1, GROUPS // 2) as i:
                gather(2 * i, 0, False)
                gather(2 * i + 1, 1, False)

        @block.scalar
        def _(act):
            for dst_t, src_t in ((src_sb, src_lanes), (rel_sb, rel_lanes), (dst_sb, dst_lanes), (norm_sb, norm_lanes)):
                act.dma_start(dst_t[:, :], src_t[:, :]).then_inc(edges_in, 16)
            act.dma_start(dst_g[:, :], dst_groups[:, :]).then_inc(edges_in, 16)
            for k in range(PAIRS):
                act.wait_ge(w_in[k], 16)
                nc.scalar.activation(w_split[:, 0, k], w_raw[:, k], ACT.Copy).then_inc(w_hi_done, 1)

            def evacuate(n, b, uses):
                if uses is not None:
                    act.wait_ge(stored[b], 16 * uses)
                for k in range(0, PAIRS, 2):
                    act.wait_ge(bank_done, PAIRS * n + k + 1)
                    nc.scalar.activation(stage[:, b, k * 2 * F:(k + 1) * 2 * F], bank[k][:, :],
                                         ACT.Copy).then_inc(evac_act, 1)

            act.wait_ge(w_lo_done, PAIRS)
            evacuate(0, 0, None)
            evacuate(1, 1, None)
            evacuate(2, 0, 1)
            with act.Fori(1, TILES // 2) as i:
                evacuate(2 * i + 1, 1, i)
                evacuate(2 * i + 2, 0, i + 1)

            def name_rows(g, b):
                act.copy(row_now[:, b * GROUP:(b + 1) * GROUP], col(row_sb, g * GROUP, GROUP)).then_inc(row_now_done, 1)

            act.wait_ge(rows_named, 1)
            name_rows(0, 0)
            name_rows(1, 1)

            def scale(g, b, uses, more, first=False):
                if not first:
                    act.wait_ge(onehot_first, g)
                for j in range(GROUP):
                    s = b * GROUP + j
                    act.wait_ge(gathered[s], 16 * (uses + 1))
                    nc.scalar.activation(msg[:, 0, s, :], rows[:, s, :], ACT.Copy,
                                         scale=col(norm_sb, g * GROUP + j)).then_inc(hi_done, 1)
                if more:
                    name_rows(g + 2, b)

            scale(0, 0, 0, True, first=True)
            scale(1, 1, 0, True)
            with act.Fori(1, GROUPS // 2 - 1) as i:
                scale(2 * i, 0, i, True)
                scale(2 * i + 1, 1, i, True)
            scale(GROUPS - 2, 0, GROUPS // 2 - 1, False)
            scale(GROUPS - 1, 1, GROUPS // 2 - 1, False)

            act.wait_ge(stats_done, 2 * TILES)
            nc.scalar.activation(std[:, :], mean_var[:, :, 1], ACT.Sqrt, bias=eps[:, 0:1]).then_inc(std_done, 1)
            act.wait_ge(rstd_done, 2)
            for t in range(1, TILES, 2):
                nc.scalar.activation(acc[:, t, :], acc[:, t, :], ACT.Identity, bias=shift[:, t:t + 1],
                                     scale=rstd[:, t:t + 1]).then_inc(norm_act, 1)

        @block.vector
        def _(dve):
            def split_x(n, b, uses):
                dve.wait_ge(x_in[b], 16 * (uses + 1))
                nc.vector.tensor_copy(x_split[:, b, 0], x_raw[:, b]).then_inc(x_hi_done, 1)
                dve.wait_ge(x_hi_done, n + 1)
                nc.vector.tensor_tensor(x_split[:, b, 1], x_raw[:, b], x_split[:, b, 0].bitcast(f32),
                                        ALU.subtract).then_inc(x_lo_done, 1)

            def evacuate(n, b, uses):
                if uses is not None:
                    dve.wait_ge(stored[b], 16 * uses)
                for k in range(1, PAIRS, 2):
                    dve.wait_ge(bank_done, PAIRS * n + k + 1)
                    nc.vector.tensor_copy(stage[:, b, k * 2 * F:(k + 1) * 2 * F],
                                          bank[k][:, :]).then_inc(evac_dve, 1)

            split_x(0, 0, 0)
            for k in range(PAIRS):
                dve.wait_ge(w_hi_done, k + 1)
                nc.vector.tensor_tensor(w_split[:, 1, k], w_raw[:, k], w_split[:, 0, k].bitcast(f32),
                                        ALU.subtract).then_inc(w_lo_done, 1)
            split_x(1, 1, 0)
            dve.wait_ge(w_lo_done, PAIRS)
            evacuate(0, 0, None)

            dve.wait_ge(edges_in, 16 * 5)
            nc.vector.scalar_tensor_tensor(out=row_sb[:, :], in0=src_sb[:, :], scalar=float(RELS),
                                           in1=rel_sb[:, :], op0=ALU.mult, op1=ALU.add).then_inc(rows_named, 1)
            nc.vector.tensor_copy(dst_f[:, :], dst_sb[:, :]).then_inc(consts, 1)
            nc.vector.tensor_reduce(span[:, 0:1], dst_g[:, :], AX.X, ALU.min).then_inc(span_done, 1)
            nc.vector.tensor_reduce(span[:, 1:2], dst_g[:, :], AX.X, ALU.max).then_inc(span_done, 1)
            dve.wait_ge(span_done, 2)
            nc.vector.tensor_single_scalar(span_tile[:, :], span[:, :], P.bit_length() - 1,
                                           ALU.arith_shift_right).then_inc(span_done, 2)

            def tile_step(n, b, i, uses):
                dve.wait_ge(bank_done, PAIRS * n)
                split_x(n + 1, 1 - b, i + 1)
                evacuate(n, b, uses)

            tile_step(1, 1, 0, None)
            tile_step(2, 0, 0, 1)
            with dve.Fori(1, TILES // 2 - 1) as i:
                tile_step(2 * i + 1, 1, i, i)
                tile_step(2 * i + 2, 0, i, i + 1)
            n = TILES - 2
            dve.wait_ge(bank_done, PAIRS * n)
            split_x(n + 1, 0, TILES // 2)
            evacuate(n, 1, TILES // 2 - 1)
            evacuate(n + 1, 0, TILES // 2)

            more = dve.alloc_register("dve_more")
            dve.reg_mov(more, 0)
            rel_count = dve.alloc_register("dve_rel_count")
            dve.reg_mov(rel_count, 0)

            def open_tile(g, t, opened):
                nc.vector.tensor_scalar(dst_rel[:, :], col(dst_f, g * GROUP, GROUP), col(tile_base, t),
                                        None, ALU.subtract).then_inc(dst_rel_done, 1)
                dve.reg_add(rel_count, rel_count, 1)
                dve.wait_ge(dst_rel_done, dve.snap(rel_count))
                nc.vector.tensor_tensor(onehot[:, :, :],
                                        lane[:, :].rearrange("p (a n) -> p a n", a=1).to_broadcast([P, GROUP, P]),
                                        dst_rel[:, :].rearrange("p (g a) -> p g a", a=1).to_broadcast([P, GROUP, P]),
                                        ALU.is_equal).then_inc(opened, 1)

            def add_tile(g, b, t):
                nc.vector.tensor_tensor(acc[:, bass.ds(t, 1), :].rearrange("p a f -> p (a f)"),
                                        acc[:, bass.ds(t, 1), :].rearrange("p a f -> p (a f)"),
                                        bank[b][:, 0:F], ALU.add).then_inc(acc_done, 1)

            def group(g, b):
                lo = dve.value_load(ranges[0:1, bass.ds(2 * g, 1)], min_val=0, max_val=TILES - 1)
                hi = dve.value_load(ranges[0:1, bass.ds(2 * g + 1, 1)], min_val=0, max_val=TILES - 1)
                open_tile(g, lo, onehot_first)
                for j in range(GROUP):
                    s = b * GROUP + j
                    dve.wait_ge(hi_done, GROUP * g + j + 1)
                    nc.vector.scalar_tensor_tensor(out=msg[:, 1, s, :], in0=rows[:, s, :],
                                                   scalar=col(norm_sb, g * GROUP + j),
                                                   in1=msg[:, 0, s, :].bitcast(f32),
                                                   op0=ALU.mult, op1=ALU.subtract).then_inc(lo_done, 1)
                dve.wait_ge(sum_first, g + 1)
                add_tile(g, b, lo)
                with dve.If(lo < hi):
                    with dve.Fori(lo + 1, hi + 1) as t:
                        open_tile(g, t, onehot_more)
                        dve.reg_add(more, more, 1)
                        dve.wait_ge(sum_more, dve.snap(more))
                        add_tile(g, b, t)

            dve.wait_ge(consts, 4)
            dve.wait_ge(acc_in, 16)
            dve.wait_ge(ranges_in, 16)
            with dve.Fori(0, GROUPS // 2) as i:
                group(2 * i, 0)
                group(2 * i + 1, 1)

            dve.wait_ge(acc_done, dve.snap(more) + GROUPS)
            for t in range(TILES):
                nc.vector.bn_stats(stats[:, t, :], acc[:, t, :]).then_inc(stats_done, 1)
            dve.wait_ge(stats_done, TILES)
            for t in range(TILES):
                nc.vector.bn_aggr(mean_var[:, t, :], stats[:, t, :]).then_inc(stats_done, 1)
            dve.wait_ge(std_done, 1)
            nc.vector.reciprocal(rstd[:, :], std[:, :]).then_inc(rstd_done, 1)
            dve.wait_ge(rstd_done, 1)
            nc.vector.scalar_tensor_tensor(out=shift[:, :], in0=mean_var[:, :, 0], scalar=-1.0,
                                           in1=rstd[:, :], op0=ALU.mult, op1=ALU.mult).then_inc(rstd_done, 1)
            for t in range(0, TILES, 2):
                nc.vector.tensor_scalar(acc[:, t, :], acc[:, t, :], mean_var[:, t, 0:1], rstd[:, t:t + 1],
                                        ALU.subtract, ALU.mult).then_inc(norm_dve, 1)

        @block.tensor
        def _(pe):
            PARTS = ((0, 0), (0, 1), (1, 0))

            def transform(n, b, first):
                pe.wait_ge(x_lo_done, n + 1)
                for k in range(PAIRS):
                    if first:
                        pe.wait_ge(w_lo_done, k + 1)
                    else:
                        evac = evac_dve if k % 2 else evac_act
                        pe.wait_ge(evac, (PAIRS // 2) * (n - 1) + k // 2 + 1)
                    steps = [(a, c, h) for a, c in PARTS for h in range(HALVES)]
                    for m, (a, c, h) in enumerate(steps):
                        last = nc.tensor.matmul(bank[k][:, :], x_split[:, b, a, h], w_split[:, c, k, h],
                                                start=m == 0, stop=m == len(steps) - 1)
                    last.then_inc(bank_done, 1)

            transform(0, 0, True)
            with pe.Fori(0, TILES // 2) as i:
                transform(2 * i + 1, 1, False)
                transform(2 * i + 2, 0, False)

            more = pe.alloc_register("pe_more")
            pe.reg_mov(more, 0)

            def sum_chunk(b, j, last_inc):
                s = b * GROUP + j
                for a in range(2):
                    last = nc.tensor.matmul(bank[b][:, 0:F], onehot[:, j, :], msg[:, a, s, :],
                                            start=j == 0 and a == 0, stop=j == GROUP - 1 and a == 1)
                if j == GROUP - 1:
                    last.then_inc(last_inc, 1)

            def group(g, b):
                lo = pe.value_load(ranges[0:1, bass.ds(2 * g, 1)], min_val=0, max_val=TILES - 1)
                hi = pe.value_load(ranges[0:1, bass.ds(2 * g + 1, 1)], min_val=0, max_val=TILES - 1)
                pe.wait_ge(onehot_first, g + 1)
                for j in range(GROUP):
                    pe.wait_ge(lo_done, GROUP * g + j + 1)
                    sum_chunk(b, j, sum_first)
                with pe.If(lo < hi):
                    with pe.Fori(lo + 1, hi + 1):
                        pe.reg_add(more, more, 1)
                        pe.wait_ge(onehot_more, pe.snap(more))
                        for j in range(GROUP):
                            sum_chunk(b, j, sum_more)

            pe.wait_ge(evac_act, (PAIRS // 2) * TILES)
            pe.wait_ge(evac_dve, (PAIRS // 2) * TILES)
            pe.wait_ge(ranges_in, 16)
            with pe.Fori(0, GROUPS // 2) as i:
                group(2 * i, 0)
                group(2 * i + 1, 1)


def kernel(x, src, dst, edge_type_16, edge_weight1, L0_gnn_weight):
    import numpy as np
    import concourse.bacc as bacc
    from concourse.bass_utils import run_bass_kernel_spmd

    x, w = np.asarray(x), np.asarray(L0_gnn_weight)
    nodes, feats = x.shape
    rels = w.shape[0]
    edges = np.asarray(src).shape[0]
    tiles = -(-nodes // P)
    group = 8
    chunks = -(-edges // (P * 2 * group)) * 2 * group
    x_rows = np.concatenate([x, np.zeros((tiles * P - nodes, feats), x.dtype)])

    def padded(a, fill):
        a = np.asarray(a).reshape(-1)
        return np.concatenate([a, np.full(chunks * P - edges, fill, a.dtype)])

    def lanes(a):
        return np.ascontiguousarray(a.reshape(chunks, P).T)

    dst_flat = padded(dst, nodes - 1)
    arrays = {
        "x_rows": x_rows,
        "x_cols": np.ascontiguousarray(x_rows.T),
        "weight": np.ascontiguousarray(w.reshape(rels // 2, 2, feats // P, P, feats).transpose(0, 3, 2, 1, 4))
                    .reshape(rels // 2, P, -1),
        "src_lanes": lanes(padded(src, 0)),
        "rel_lanes": lanes(padded(edge_type_16, 0)),
        "dst_lanes": lanes(dst_flat),
        "norm_lanes": lanes(padded(edge_weight1, 0)),
        "dst_groups": dst_flat.reshape(chunks // group, group * P),
    }
    nc = bacc.Bacc("TRN2", target_bir_lowering=False, num_devices=1)
    args = [nc.dram_tensor(n, a.shape, mybir.dt.from_np(a.dtype), kind="ExternalInput").ap()
            for n, a in arrays.items()]
    out = nc.dram_tensor("out", (nodes, feats), mybir.dt.float32, kind="ExternalOutput").ap()
    resnorm_gnn(nc, *args, out)
    result = run_bass_kernel_spmd(nc, [arrays], core_ids=[0])
    return result.results[0]["out"]
```

```python
import concourse.bass as bass
from concourse import mybir
from contextlib import ExitStack


P = 128
EPS = 1e-5


def resnorm_gnn(nc, x_cols, weight, src_lanes, rel_lanes, dst_lanes, norm_lanes,
                dst_groups, out):
    f32, f32r, i32 = mybir.dt.float32, mybir.dt.float32r, mybir.dt.int32
    ALU, ACT, AX = mybir.AluOpType, mybir.ActivationFunctionType, mybir.AxisListType

    NODES, F = out.shape
    RELS = 2 * weight.shape[0]
    TILES = x_cols.shape[1] // P
    HALVES = F // P
    PAIRS = RELS // 2
    CHUNKS = src_lanes.shape[1]
    GROUP = 8
    HALF_GROUP = GROUP // 2
    GROUPS = CHUNKS // GROUP
    RING = 4
    SLOTS = RING * GROUP
    BATCH = 4
    BATCHES = TILES // BATCH
    ROW = RELS * F
    LAST = NODES - (TILES - 1) * P
    assert TILES % (2 * BATCH) == 1 and GROUPS % RING == 2

    table = nc.dram_tensor("table", [TILES * P * RELS, F], f32).ap()
    first_dram = nc.dram_tensor("first_dram", [GROUPS, 1], i32).ap()
    further_dram = nc.dram_tensor("further_dram", [GROUPS, 1], i32).ap()
    table_tiles = table.rearrange("(t p r) f -> t p (r f)", p=P, r=RELS)
    xc = x_cols.rearrange("(h p) n -> p h n", p=P)

    ctx = ExitStack()
    with ctx:
        def sb(name, shape, dt):
            return ctx.enter_context(nc.sbuf_tensor(name, shape, dt))

        def sem(name):
            return ctx.enter_context(nc.semaphore(name))

        stage = sb("stage", [P, 2, ROW], f32)
        w_raw = stage[:, :, :].rearrange("p a (k h n) -> p (a k) h n", h=HALVES, n=2 * F)
        rows = stage[:, :, :].rearrange("p a (s f) -> p (a s) f", f=F)
        w_split = sb("w_split", [P, 2, PAIRS, HALVES, 2 * F], f32r)
        MSGS = 2 * GROUP
        msg = w_split[:, :, :, :, :].rearrange("p a k h (two f) -> p a (k h two) f", two=2)
        onehot = sb("onehot", [P, 2, GROUP, P], f32r)
        x_raw = sb("x_raw", [P, 2, HALVES, P], f32)
        x_split = sb("x_split", [P, 2, 2, HALVES, P], f32r)
        acc = sb("acc", [P, HALVES, (TILES + 1) * P], f32)
        src_sb = sb("src_sb", [P, CHUNKS], i32)
        rel_sb = sb("rel_sb", [P, CHUNKS], i32)
        row_sb = sb("row_sb", [P, CHUNKS], i32)
        dst_sb = sb("dst_sb", [P, CHUNKS], i32)
        dst_off = sb("dst_off", [P, CHUNKS], f32)
        norm_sb = sb("norm_sb", [P, CHUNKS], f32)
        dst_rel = sb("dst_rel", [P, GROUP], f32)
        row_now = sb("row_now", [P, SLOTS], i32)
        norm_now = sb("norm_now", [P, SLOTS], f32)
        lane = sb("lane", [P, P], f32)
        window_base = sb("window_base", [P, TILES], f32)
        ident = sb("ident", [P, P], f32)
        first_all = sb("first_all", [P, GROUPS], i32)
        dst_g = sb("dst_g", [GROUPS, GROUP * P], i32)
        span = sb("span", [GROUPS, 3], i32)
        further_col = sb("further_col", [GROUPS, 1], i32)
        further = sb("further", [1, GROUPS], i32)
        stats = sb("stats", [P, 2, BATCH, 6], f32)
        mean_var = sb("mean_var", [P, 2, BATCH, 2], f32)
        std = sb("std", [P, 2, BATCH], f32)
        rstd = sb("rstd", [P, 2, BATCH], f32)
        shift = sb("shift", [P, 2, BATCH], f32)
        out_sb = rows[:, 0:2 * BATCH, :]
        eps = sb("eps", [P, 1], f32)

        psum = ctx.enter_context(nc.psum_tensor("psum", [P, PAIRS, 2 * F], f32))
        bank = [psum[:, k, :] for k in range(PAIRS)]

        w_in = [sem(f"w_in{k}") for k in range(PAIRS)]
        x_in = [sem("x_in0"), sem("x_in1")]
        w_hi_done, w_lo_done = sem("w_hi_done"), sem("w_lo_done")
        x_hi_done, x_lo_done = sem("x_hi_done"), sem("x_lo_done")
        bank_done = sem("bank_done")
        evac_act, evac_dve = sem("evac_act"), sem("evac_dve")
        stored = [sem("stored0"), sem("stored1")]
        edges_in, acc_in = sem("edges_in"), sem("acc_in")
        consts, span_done, span_out, ranges_in = sem("consts"), sem("span_done"), sem("span_out"), sem("ranges_in")
        ident_zero, acc_tail, dst_off_done = sem("ident_zero"), sem("acc_tail"), sem("dst_off_done")
        rows_named, row_now_done, norm_now_done = sem("rows_named"), sem("row_now_done"), sem("norm_now_done")
        gathered = [sem(f"gathered{s}") for s in range(SLOTS)]
        pool_passed = sem("pool_passed")
        hi_done, lo_done = sem("hi_done"), sem("lo_done")
        dst_rel_done = sem("dst_rel_done")
        onehot_first, onehot_more = sem("onehot_first"), sem("onehot_more")
        sum_first, sum_more = sem("sum_first"), sem("sum_more")
        all_added = sem("all_added")
        acc_done, turned = sem("acc_done"), sem("turned")
        stats_done, aggr_done, std_done, rstd_done = sem("stats_done"), sem("aggr_done"), sem("std_done"), sem("rstd_done")
        shift_done, stats_seen = sem("shift_done"), sem("stats_seen")
        norm_dve, norm_act = sem("norm_dve"), sem("norm_act")
        out_done = [sem("out_done0"), sem("out_done1")]

        block = ctx.enter_context(nc.Block())

        def col(t, i, n=1):
            return t[:, bass.ds(i, n)]


        @block.sync
        def _(sp):
            def load_x(n, b):
                sp.dma_start(x_raw[:, b], xc[:, :, bass.ds(n * P, P)]).then_inc(x_in[b], 16)

            def store(n, b):
                sp.wait_ge(evac_act, (PAIRS // 2) * (n + 1))
                sp.wait_ge(evac_dve, (PAIRS // 2) * (n + 1))
                sp.dma_start(table_tiles[bass.ds(n, 1)].rearrange("a p n -> (a p) n"),
                             stage[:, b]).then_inc(stored[b], 16)

            load_x(0, 0)
            for k in range(PAIRS):
                sp.dma_start(w_raw[:, k].rearrange("p h n -> p (h n)"), weight[k]).then_inc(w_in[k], 16)
                if k == 0:
                    load_x(1, 1)
            sp.dma_start(acc[:, :, 0:TILES * P], xc).then_inc(acc_in, 16)
            sp.wait_ge(x_lo_done, 1)
            load_x(2, 0)
            store(0, 0)
            with sp.Fori(0, TILES // 2 - 1) as i:
                for b in (1, 0):
                    n = 2 * i + 2 - b
                    sp.wait_ge(x_lo_done, n + 1)
                    load_x(n + 2, b)
                    store(n, b)
            for n, b in ((TILES - 2, 1), (TILES - 1, 0)):
                store(n, b)
            sp.wait_ge(span_done, 4)
            sp.dma_start(first_dram[:, :], span[:, 0:1]).then_inc(span_out, 16)
            sp.dma_start(further_dram[:, :], further_col[:, :]).then_inc(span_out, 16)
            sp.wait_ge(span_out, 32)
            sp.dma_start(first_all[:, :], first_dram.rearrange("g a -> a g").to_broadcast([P, GROUPS])).then_inc(ranges_in, 16)
            sp.dma_start(further[:, :], further_dram.rearrange("g a -> a g")).then_inc(ranges_in, 16)

            def store_out(q, b):
                sp.wait_ge(norm_dve, (BATCH // 2) * (q + 1))
                sp.wait_ge(norm_act, (BATCH // 2) * (q + 1))
                sp.dma_start(out[bass.ds(q * BATCH * P, BATCH * P), :].rearrange("(t p) f -> p t f", p=P),
                             out_sb[:, b * BATCH:(b + 1) * BATCH, :]).then_inc(out_done[b], 16)

            with sp.Fori(0, BATCHES // 2) as i:
                store_out(2 * i, 0)
                store_out(2 * i + 1, 1)
            sp.wait_ge(norm_dve, (BATCH // 2) * BATCHES + 1)
            sp.dma_start(out[(TILES - 1) * P:NODES, :], out_sb[0:LAST, 0, :]).then_inc(out_done[0], 16)
            sp.wait_ge(out_done[0], 16 * (BATCHES // 2 + 1))
            sp.wait_ge(out_done[1], 16 * (BATCHES // 2))

        @block.gpsimd
        def _(pool):
            pool.iota(lane[:, :], pattern=[[1, P]], base=0, channel_multiplier=0,
                      allow_small_or_imprecise_dtypes=True).then_inc(consts, 1)
            pool.iota(window_base[:, :], pattern=[[P, TILES]], base=0, channel_multiplier=0,
                      allow_small_or_imprecise_dtypes=True).then_inc(consts, 1)
            pool.memset(eps[:, :], EPS).then_inc(consts, 1)
            pool.memset(acc[:, :, TILES * P:], 0.0).then_inc(acc_tail, 1)
            pool.memset(ident[:, :], 0.0).then_inc(ident_zero, 1)
            pool.wait_ge(ident_zero, 1)
            pool.affine_select(out=ident[:, :], in_=ident[:, :], compare_op=ALU.not_equal, fill=1.0, base=0,
                               pattern=[[-1, P]], channel_multiplier=1).then_inc(consts, 1)

            def gather(g, r):
                pool.wait_ge(row_now_done, g + 1)
                pool.sem_inc(pool_passed, 1)
                for j in range(GROUP):
                    s = r * GROUP + j
                    pool.indirect_dma_start(
                        out=rows[:, s, :], out_offset=None, in_=table[:, :],
                        in_offset=bass.IndirectOffsetOnAxis(ap=row_now[:, s:s + 1], axis=0),
                    ).then_inc(gathered[s], 16)

            pool.wait_ge(stored[0], 16 * (TILES // 2 + 1))
            pool.wait_ge(stored[1], 16 * (TILES // 2))
            gather(0, 0)
            gather(1, 1)
            with pool.Fori(0, GROUPS // RING) as i:
                for u in range(RING):
                    gather(RING * i + 2 + u, (2 + u) % RING)

        @block.scalar
        def _(act):
            for dst_t, src_t in ((src_sb, src_lanes), (rel_sb, rel_lanes), (dst_sb, dst_lanes), (norm_sb, norm_lanes)):
                act.dma_start(dst_t[:, :], src_t[:, :]).then_inc(edges_in, 16)
            act.dma_start(dst_g[:, :], dst_groups[:, :]).then_inc(edges_in, 16)
            for k in range(PAIRS):
                act.wait_ge(w_in[k], 16)
                nc.scalar.activation(w_split[:, 0, k], w_raw[:, k], ACT.Copy).then_inc(w_hi_done, 1)

            def evacuate(n, b, uses):
                if uses is not None:
                    act.wait_ge(stored[b], 16 * uses)
                for k in range(0, PAIRS, 2):
                    act.wait_ge(bank_done, PAIRS * n + k + 1)
                    nc.scalar.activation(stage[:, b, k * 2 * F:(k + 1) * 2 * F], bank[k],
                                         ACT.Copy).then_inc(evac_act, 1)

            act.wait_ge(w_lo_done, PAIRS)
            evacuate(0, 0, None)
            evacuate(1, 1, None)
            evacuate(2, 0, 1)
            with act.Fori(1, TILES // 2) as i:
                evacuate(2 * i + 1, 1, i)
                evacuate(2 * i + 2, 0, i + 1)

            def name_rows(g, r):
                act.copy(row_now[:, r * GROUP:(r + 1) * GROUP], col(row_sb, g * GROUP, GROUP)).then_inc(row_now_done, 1)
                act.copy(norm_now[:, r * GROUP:(r + 1) * GROUP], col(norm_sb, g * GROUP, GROUP)).then_inc(norm_now_done, 1)

            def scale(g, r, uses, more, first=False):
                act.wait_ge(norm_now_done, g + 1)
                if more and not first:
                    act.wait_ge(lo_done, GROUP * (g - 1))
                if more:
                    name_rows(g + 2, (r + 2) % RING)
                act.wait_ge(onehot_first, g + 1)
                for j in range(GROUP):
                    s = r * GROUP + j
                    act.wait_ge(gathered[s], 16 * (uses + 1))
                    nc.scalar.activation(msg[:, 0, s % MSGS, :], rows[:, s, :], ACT.Copy,
                                         scale=norm_now[:, s:s + 1]).then_inc(hi_done, 1)

            act.wait_ge(rows_named, 1)
            name_rows(0, 0)
            name_rows(1, 1)
            scale(0, 0, 0, True, first=True)
            scale(1, 1, 0, True, first=True)
            scale(2, 2, 0, True)
            scale(3, 3, 0, True)
            with act.Fori(1, GROUPS // RING) as i:
                for u in range(RING):
                    scale(RING * i + u, u, i, True)
            for g in (GROUPS - 2, GROUPS - 1):
                scale(g, g % RING, GROUPS // RING, False)

            def normalise(q, b, uses, tiles):
                act.wait_ge(aggr_done, q * BATCH + tiles)
                nc.scalar.activation(std[:, b, 0:tiles], mean_var[:, b, 0:tiles, 1], ACT.Sqrt,
                                     bias=eps[:, 0:1]).then_inc(std_done, 1)
                if tiles == 1:
                    return
                if uses is not None:
                    act.wait_ge(out_done[b], 16 * uses)
                act.wait_ge(shift_done, q + 1)
                for t in range(1, BATCH, 2):
                    nc.scalar.activation(out_sb[:, b * BATCH + t, :], bank[b * BATCH + t][:, 0:F], ACT.Identity,
                                         bias=shift[:, b, t:t + 1], scale=rstd[:, b, t:t + 1]).then_inc(norm_act, 1)

            normalise(0, 0, None, BATCH)
            normalise(1, 1, None, BATCH)
            with act.Fori(1, BATCHES // 2) as i:
                normalise(2 * i, 0, i, BATCH)
                normalise(2 * i + 1, 1, i, BATCH)
            normalise(BATCHES, 0, BATCHES // 2, 1)

        @block.vector
        def _(dve):
            def split_x(n, b, uses):
                dve.wait_ge(x_in[b], 16 * (uses + 1))
                nc.vector.tensor_copy(x_split[:, b, 0], x_raw[:, b]).then_inc(x_hi_done, 1)
                dve.wait_ge(x_hi_done, n + 1)
                nc.vector.tensor_tensor(x_split[:, b, 1], x_raw[:, b], x_split[:, b, 0].bitcast(f32),
                                        ALU.subtract).then_inc(x_lo_done, 1)

            def evacuate(n, b, uses):
                if uses is not None:
                    dve.wait_ge(stored[b], 16 * uses)
                for k in range(1, PAIRS, 2):
                    dve.wait_ge(bank_done, PAIRS * n + k + 1)
                    nc.vector.tensor_copy(stage[:, b, k * 2 * F:(k + 1) * 2 * F],
                                          bank[k]).then_inc(evac_dve, 1)

            split_x(0, 0, 0)
            for k in range(PAIRS):
                dve.wait_ge(w_hi_done, k + 1)
                nc.vector.tensor_tensor(w_split[:, 1, k], w_raw[:, k], w_split[:, 0, k].bitcast(f32),
                                        ALU.subtract).then_inc(w_lo_done, 1)
            split_x(1, 1, 0)
            dve.wait_ge(w_lo_done, PAIRS)
            evacuate(0, 0, None)

            dve.wait_ge(edges_in, 16 * 5)
            nc.vector.scalar_tensor_tensor(out=row_sb[:, :], in0=src_sb[:, :], scalar=float(RELS),
                                           in1=rel_sb[:, :], op0=ALU.mult, op1=ALU.add).then_inc(rows_named, 1)
            nc.vector.tensor_reduce(span[:, 0:1], dst_g[:, :], AX.X, ALU.min).then_inc(span_done, 1)
            nc.vector.tensor_reduce(span[:, 1:2], dst_g[:, :], AX.X, ALU.max).then_inc(span_done, 1)
            dve.wait_ge(span_done, 2)
            nc.vector.tensor_tensor(span[:, 2:3], span[:, 1:2], span[:, 0:1], ALU.subtract).then_inc(span_done, 1)
            dve.wait_ge(span_done, 3)
            nc.vector.tensor_single_scalar(further_col[:, :], span[:, 2:3], P.bit_length() - 1,
                                           ALU.arith_shift_right).then_inc(span_done, 1)

            def tile_step(n, b, i, uses):
                dve.wait_ge(bank_done, PAIRS * n)
                split_x(n + 1, 1 - b, i + 1)
                evacuate(n, b, uses)

            tile_step(1, 1, 0, None)
            tile_step(2, 0, 0, 1)
            with dve.Fori(1, TILES // 2 - 1) as i:
                tile_step(2 * i + 1, 1, i, i)
                tile_step(2 * i + 2, 0, i, i + 1)
            n = TILES - 2
            dve.wait_ge(bank_done, PAIRS * n)
            split_x(n + 1, 0, TILES // 2)
            evacuate(n, 1, TILES // 2 - 1)
            evacuate(n + 1, 0, TILES // 2)

            more = dve.alloc_register("dve_more")
            dve.reg_mov(more, 0)

            def lane_is(offsets, b, opened):
                nc.vector.tensor_tensor(onehot[:, b, :, :],
                                        lane[:, :].rearrange("p (a n) -> p a n", a=1).to_broadcast([P, GROUP, P]),
                                        offsets.rearrange("p (g a) -> p g a", a=1).to_broadcast([P, GROUP, P]),
                                        ALU.is_equal).then_inc(opened, 1)

            def add_window(node, b):
                place = acc[:, :, bass.ds(node, P)]
                nc.vector.tensor_tensor(place, place, psum[:, HALVES * b:HALVES * (b + 1), 0:P],
                                        ALU.add).then_inc(acc_done, 1)

            def split_group(g, r):
                lane_is(col(dst_off, g * GROUP, GROUP), r % 2, onehot_first)
                for j in range(GROUP):
                    s = r * GROUP + j
                    if j % 2 == 0:
                        dve.wait_ge(hi_done, GROUP * g + j + 2)
                    nc.vector.scalar_tensor_tensor(out=msg[:, 1, s % MSGS, :], in0=rows[:, s, :],
                                                   scalar=norm_now[:, s:s + 1],
                                                   in1=msg[:, 0, s % MSGS, :].bitcast(f32),
                                                   op0=ALU.mult, op1=ALU.subtract).then_inc(lo_done, 1)

            def finish_group(g, b, very_first=False):
                node = dve.value_load(first_all[0:1, bass.ds(g, 1)], min_val=0, max_val=NODES - 1)
                windows = dve.value_load(further[0:1, bass.ds(g, 1)], min_val=0, max_val=TILES - 1)
                added = dve.snap(more) + g
                dve.wait_ge(sum_first, g + 1)
                if not very_first:
                    dve.wait_ge(acc_done, added)
                add_window(node, b)
                with dve.If(windows > 0):
                    with dve.Fori(1, windows + 1) as w:
                        nc.vector.tensor_scalar(dst_rel[:, :], col(dst_off, g * GROUP, GROUP), col(window_base, w),
                                                None, ALU.subtract).then_inc(dst_rel_done, 1)
                        dve.reg_add(more, more, 1)
                        count = dve.snap(more)
                        dve.wait_ge(dst_rel_done, count)
                        lane_is(dst_rel[:, :], b, onehot_more)
                        dve.wait_ge(sum_more, count)
                        dve.wait_ge(acc_done, count + g)
                        add_window(nc.s_assert_within(node + w * P, 0, NODES - 1), b)

            dve.wait_ge(consts, 4)
            dve.wait_ge(acc_in, 16)
            dve.wait_ge(acc_tail, 1)
            dve.wait_ge(ranges_in, 32)
            nc.vector.tensor_tensor(dst_off[:, :].rearrange("p (g c) -> p g c", c=GROUP),
                                    dst_sb[:, :].rearrange("p (g c) -> p g c", c=GROUP),
                                    first_all[:, :].rearrange("p (g a) -> p g a", a=1).to_broadcast([P, GROUPS, GROUP]),
                                    ALU.subtract).then_inc(dst_off_done, 1)
            dve.wait_ge(dst_off_done, 1)
            split_group(0, 0)
            split_group(1, 1)
            finish_group(0, 0, very_first=True)
            with dve.Fori(0, GROUPS // RING) as i:
                for u in range(RING):
                    split_group(RING * i + 2 + u, (2 + u) % RING)
                    finish_group(RING * i + 1 + u, (1 + u) % 2)
            finish_group(GROUPS - 1, 1)
            dve.wait_ge(acc_done, dve.snap(more) + GROUPS)
            dve.sem_inc(all_added, 1)

            def normalise(q, b, uses, tiles):
                for t in range(tiles):
                    dve.wait_ge(turned, q * BATCH + t + 1)
                    nc.vector.bn_stats(stats[:, b, t, :], bank[b * BATCH + t][:, 0:F]).then_inc(stats_done, 1)
                dve.wait_ge(stats_done, q * BATCH + tiles)
                dve.sem_inc(stats_seen, 1)
                for t in range(tiles):
                    nc.vector.bn_aggr(mean_var[:, b, t, :], stats[:, b, t, :]).then_inc(aggr_done, 1)
                dve.wait_ge(std_done, q + 1)
                nc.vector.reciprocal(rstd[:, b, 0:tiles], std[:, b, 0:tiles]).then_inc(rstd_done, 1)
                dve.wait_ge(rstd_done, q + 1)
                nc.vector.scalar_tensor_tensor(out=shift[:, b, 0:tiles], in0=mean_var[:, b, 0:tiles, 0], scalar=-1.0,
                                               in1=rstd[:, b, 0:tiles], op0=ALU.mult, op1=ALU.mult).then_inc(shift_done, 1)
                if uses is not None:
                    dve.wait_ge(out_done[b], 16 * uses)
                for t in range(0, tiles, 2):
                    nc.vector.tensor_scalar(out_sb[:, b * BATCH + t, :], bank[b * BATCH + t][:, 0:F],
                                            mean_var[:, b, t, 0:1], rstd[:, b, t:t + 1],
                                            ALU.subtract, ALU.mult).then_inc(norm_dve, 1)

            normalise(0, 0, None, BATCH)
            normalise(1, 1, None, BATCH)
            with dve.Fori(1, BATCHES // 2) as i:
                normalise(2 * i, 0, i, BATCH)
                normalise(2 * i + 1, 1, i, BATCH)
            normalise(BATCHES, 0, BATCHES // 2, 1)

        @block.tensor
        def _(pe):
            PARTS = ((0, 0), (0, 1), (1, 0))

            def transform(n, b, first):
                pe.wait_ge(x_lo_done, n + 1)
                for k in range(PAIRS):
                    if first:
                        pe.wait_ge(w_lo_done, k + 1)
                    else:
                        evac = evac_dve if k % 2 else evac_act
                        pe.wait_ge(evac, (PAIRS // 2) * (n - 1) + k // 2 + 1)
                    steps = [(a, c, h) for a, c in PARTS for h in range(HALVES)]
                    for m, (a, c, h) in enumerate(steps):
                        last = nc.tensor.matmul(bank[k], x_split[:, b, a, h], w_split[:, c, k, h],
                                                start=m == 0, stop=m == len(steps) - 1)
                    last.then_inc(bank_done, 1)

            transform(0, 0, True)
            with pe.Fori(0, TILES // 2) as i:
                transform(2 * i + 1, 1, False)
                transform(2 * i + 2, 0, False)

            more = pe.alloc_register("pe_more")
            pe.reg_mov(more, 0)

            def sum_chunk(b, j, done):
                s = b * GROUP + j
                for h in range(HALVES):
                    for a in range(2):
                        last = nc.tensor.matmul(psum[:, HALVES * b + h, 0:P], msg[:, a, s, h * P:(h + 1) * P],
                                                onehot[:, b, j, :], start=j == 0 and a == 0,
                                                stop=j == GROUP - 1 and a == 1)
                if j == GROUP - 1:
                    last.then_inc(done, 1)

            def group(g, b):
                windows = pe.value_load(further[0:1, bass.ds(g, 1)], min_val=0, max_val=TILES - 1)
                pe.wait_ge(onehot_first, g + 1)
                for j in range(GROUP):
                    if j % 2 == 0:
                        pe.wait_ge(lo_done, GROUP * g + j + 2)
                    sum_chunk(b, j, sum_first)
                with pe.If(windows > 0):
                    with pe.Fori(1, windows + 1):
                        pe.reg_add(more, more, 1)
                        pe.wait_ge(onehot_more, pe.snap(more))
                        for j in range(GROUP):
                            sum_chunk(b, j, sum_more)

            pe.wait_ge(evac_act, (PAIRS // 2) * TILES)
            pe.wait_ge(evac_dve, (PAIRS // 2) * TILES)
            pe.wait_ge(ranges_in, 32)
            with pe.Fori(0, GROUPS // 2) as i:
                group(2 * i, 0)
                group(2 * i + 1, 1)

            def turn(q, b, tiles, first):
                for t in range(tiles):
                    if not first:
                        pe.wait_ge(norm_act if t % 2 else norm_dve, (BATCH // 2) * (q - 2) + t // 2 + 1)
                    for h in range(HALVES):
                        last = nc.tensor.transpose(bank[b * BATCH + t][:, h * P:(h + 1) * P],
                                                   acc[:, h, bass.ds((q * BATCH + t) * P, P)], ident[:, :])
                    last.then_inc(turned, 1)

            pe.wait_ge(consts, 4)
            pe.wait_ge(all_added, 1)
            for q in range(BATCHES):
                turn(q, q % 2, BATCH, q < 2)
            turn(BATCHES, 0, 1, False)


def kernel(x, src, dst, edge_type_16, edge_weight1, L0_gnn_weight):
    import numpy as np
    import concourse.bacc as bacc
    from concourse.bass_utils import run_bass_kernel_spmd

    x, w = np.asarray(x), np.asarray(L0_gnn_weight)
    nodes, feats = x.shape
    rels = w.shape[0]
    edges = np.asarray(src).shape[0]
    tiles = -(-nodes // P)
    group = 8
    chunks = -(-edges // (P * 2 * group)) * 2 * group
    x_rows = np.concatenate([x, np.zeros((tiles * P - nodes, feats), x.dtype)])

    def padded(a, fill):
        a = np.asarray(a).reshape(-1)
        return np.concatenate([a, np.full(chunks * P - edges, fill, a.dtype)])

    def lanes(a):
        return np.ascontiguousarray(a.reshape(chunks, P).T)

    dst_flat = padded(dst, nodes - 1)
    arrays = {
        "x_cols": np.ascontiguousarray(x_rows.T),
        "weight": np.ascontiguousarray(w.reshape(rels // 2, 2, feats // P, P, feats).transpose(0, 3, 2, 1, 4))
                    .reshape(rels // 2, P, -1),
        "src_lanes": lanes(padded(src, 0)),
        "rel_lanes": lanes(padded(edge_type_16, 0)),
        "dst_lanes": lanes(dst_flat),
        "norm_lanes": lanes(padded(edge_weight1, 0)),
        "dst_groups": dst_flat.reshape(chunks // group, group * P),
    }
    nc = bacc.Bacc("TRN2", target_bir_lowering=False, num_devices=1)
    args = [nc.dram_tensor(n, a.shape, mybir.dt.from_np(a.dtype), kind="ExternalInput").ap()
            for n, a in arrays.items()]
    out = nc.dram_tensor("out", (nodes, feats), mybir.dt.float32, kind="ExternalOutput").ap()
    resnorm_gnn(nc, *args, out)
    result = run_bass_kernel_spmd(nc, [arrays], core_ids=[0])
    return result.results[0]["out"]
```

```python
import concourse.bass as bass
from concourse import mybir
from contextlib import ExitStack


P = 128
EPS = 1e-5
BLOCK = 14
SEG = (3, 3, 4, 4)


def after(eng, sem, value):
    if not isinstance(value, int) or value > 0:
        eng.wait_ge(sem, value)


def resnorm_gnn(nc, x_cols, weight, src_lanes, rel_lanes, dst_lanes, norm_lanes,
                dst_blocks, out):
    f32, f32r, i32, bf16 = mybir.dt.float32, mybir.dt.float32r, mybir.dt.int32, mybir.dt.bfloat16
    ALU, ACT, AX = mybir.AluOpType, mybir.ActivationFunctionType, mybir.AxisListType

    NODES, F = out.shape
    RELS = 2 * weight.shape[0]
    TILES = x_cols.shape[1] // P
    HALVES = F // P
    PAIRS = RELS // 2
    STAGES = len(SEG)
    STAGE_RELS = RELS // STAGES
    STAGE_PAIRS = PAIRS // STAGES
    STAGE_ROWS = TILES * P * STAGE_RELS
    REL_BITS = STAGE_RELS.bit_length() - 1
    CHUNKS = src_lanes.shape[1]
    BLOCKS = CHUNKS // BLOCK
    SEG_START = [sum(SEG[:s]) for s in range(STAGES + 1)]
    GMAX = max(SEG)
    GROUPS = STAGES * BLOCKS
    RING = 4
    NAMED = 2 * RING
    ROUNDS = 7
    ROUND_GROUPS = BLOCKS // ROUNDS
    XRING = 4
    VALUES = 7
    BATCH_BLOCKS = 4
    SORT_BATCHES = BLOCKS // BATCH_BLOCKS
    VCOLS = VALUES * BLOCK
    SLICE = 8
    SCOLS = SLICE * STAGES * BLOCK
    BATCH = 8
    BATCHES = TILES // BATCH
    TROW = STAGE_RELS * F
    LAST = NODES - (TILES - 1) * P
    CONSTS = 10 + STAGES
    assert BLOCKS == ROUNDS * ROUND_GROUPS == SLICE * ROUNDS
    assert ROUND_GROUPS == NAMED
    assert TILES % (2 * BATCH) == 1 and RELS * TILES * P * P < 1 << 24 and SEG_START[-1] == BLOCK

    table = nc.dram_tensor("table", [STAGES * STAGE_ROWS, F], f32).ap()
    first_dram = nc.dram_tensor("first_dram", [BLOCKS, 1], i32).ap()
    further_dram = nc.dram_tensor("further_dram", [BLOCKS, 1], i32).ap()
    table_tiles = table.rearrange("(t p r) f -> t p (r f)", p=P, r=STAGE_RELS)
    xc = x_cols.rearrange("(h p) n -> p h n", p=P)

    PARTS = [(0, 3, 7), (0, 7, 4), (1, 1, 8),
             (1, 5, 8), (1, 1, 1), (2, 1, 7),
             (2, 5, 8), (2, 1, 2), (3, 1, 1),
             (3, 5, 8), (3, 1, 8)]
    assert [sum(n * k for q, n, k in PARTS if q == s) for s in range(STAGES)] == [TILES] * STAGES
    PARTS.append((STAGES, 1, 1))
    LEAD = 2
    LOOP = [3, 6, 9]
    LAST_ROUND = [[(p, 0, u) for p in parts for u in range(PARTS[p][2])] for parts in ((4, 5), (7, 8), (10,))]

    def beside_groups(s, it):
        if not isinstance(it, int) or it < ROUNDS - 2:
            return [(LOOP[s], it, u) for u in range(PARTS[LOOP[s]][2])]
        return LAST_ROUND[s] if it == ROUNDS - 2 else []

    SLOT_START = [0] + [sum(n * k for _, n, k in PARTS[1:p]) % XRING for p in range(1, len(PARTS))]

    def slot(part, u):
        return (SLOT_START[part] + u) % XRING

    def slot_next(part, u):
        return (u + 1) % PARTS[0][2] % XRING if part == 0 else slot(part, u + 1)

    def slot_uses(part, b):
        return len(range((b - SLOT_START[part]) % XRING, PARTS[part][2], XRING))

    def step(part, it, u):
        b = slot(part, u)
        before = sum(n * k for _, n, k in PARTS[:part])
        used = sum(PARTS[p][1] * slot_uses(p, b) for p in range(part))
        return before + PARTS[part][2] * it + u, used + slot_uses(part, b) * it + u // XRING

    def advance(part, it, u, by):
        u += by
        while u >= PARTS[part][2]:
            u -= PARTS[part][2]
            if not isinstance(it, int) or it + 1 < PARTS[part][1]:
                it = it + 1
            elif part + 1 < len(PARTS):
                part, it = part + 1, 0
            else:
                return None
        return part, it, u

    STAGE_END_USES = [[sum(n * slot_uses(p, b) for p, (q, n, _) in enumerate(PARTS) if q <= s) for b in range(XRING)]
                      for s in range(STAGES)]

    ctx = ExitStack()
    with ctx:
        def sb(name, shape, dt):
            return ctx.enter_context(nc.sbuf_tensor(name, shape, dt))

        def sem(name):
            return ctx.enter_context(nc.semaphore(name))

        w_split = sb("w_split", [P, 2, PAIRS, HALVES, 2 * F], f32r)
        stage = sb("stage", [P, XRING, TROW], f32)
        x_raw = sb("x_raw", [P, XRING, HALVES, P], f32)
        x_split = sb("x_split", [P, XRING, 2, HALVES, P], f32r)
        rows = sb("rows", [P, RING * GMAX, F], f32)
        w_raw = rows[:, :, :].rearrange("p (a s) (h n) -> p a (s h n)", a=4, h=2)
        W_RING = 4
        val = rows[:, :, :].rearrange("p s f -> p (s f)").bitcast(bf16)[:, 0:CHUNKS * VALUES].rearrange(
            "p (b v c) -> p b v c", v=VALUES, c=BLOCK)
        msg = sb("msg", [P, 2, 2, GMAX, F], f32r)
        onehot = sb("onehot", [P, 2, GMAX, P], f32r)
        acc = sb("acc", [P, HALVES, (TILES + 1) * P], f32)
        PAD = RING * GMAX
        row_s = sb("row_s", [P, CHUNKS + PAD], i32)
        norm_s = sb("norm_s", [P, CHUNKS + PAD], f32)
        off_s = sb("off_s", [P, CHUNKS + PAD], f32)
        row_now = sb("row_now", [P, NAMED * GMAX], i32)
        norm_now = sb("norm_now", [P, NAMED * GMAX], f32)
        off_now = sb("off_now", [P, NAMED * GMAX], f32)
        dst_rel = sb("dst_rel", [P, GMAX], f32)
        lane = sb("lane", [P, P], f32)
        window_base = sb("window_base", [P, TILES], f32)
        ident = sb("ident", [P, P], f32)
        first_all = sb("first_all", [P, BLOCKS], i32)
        span = sb("span", [BLOCKS, 3], i32)
        further_col = sb("further_col", [BLOCKS, 1], i32)
        first = sb("first", [1, GROUPS], i32)
        further = sb("further", [1, GROUPS], i32)
        eps = sb("eps", [P, 1], f32)
        lane_b = sb("lane_b", [P, P], bf16)
        slot_b = sb("slot_b", [P, BLOCK], bf16)
        ones_b = sb("ones_b", [P, P], bf16)
        later_b = sb("later_b", [P, P], bf16)
        cum = sb("cum", [P, BLOCKS, STAGES], f32)
        need = sb("need", [P, STAGES], f32)
        least = sb("least", [P, STAGES], f32)
        short = sb("short", [P, STAGES], f32)
        late = sb("late", [P, 1], i32)
        lane_hot = sb("lane_hot", [P, 2, P, BLOCK], bf16)
        placed = sb("placed", [P, 2, VALUES, BLOCK, BLOCK], bf16)
        behind = rows[:, :, :].rearrange("p s f -> p (s f)")[:, CHUNKS * VALUES // 2:]
        goes_on = behind[:, 0:SCOLS]
        slot_hot = behind[:, SCOLS:].bitcast(bf16)[:, 0:BATCH_BLOCKS * BLOCK * BLOCK].rearrange(
            "p (e s c) -> p e s c", s=BLOCK, c=BLOCK)
        flat = acc[:, :, :].rearrange("p h n -> p (h n)")

        def part(k, dt=f32, n=1):
            view = flat[:, k * CHUNKS:(k + n) * CHUNKS]
            return view if dt == f32 else view.bitcast(dt)

        src_i, rel_i, dst_i, norm_f = part(0, i32), part(1, i32), part(2, i32), part(3)
        key_i, low_i, srow_i, row_i, dlow_i, dhi_i, pack_i = (part(k, i32) for k in range(4, 11))
        digit_i = [part(k, i32) for k in (11, 12, 13)]
        rest1, rest2 = part(14), part(15)
        pos_f, pos_i, plane_i, pslot_i = part(11), part(12, i32), part(13, i32), part(14, i32)
        plane_b, pslot_b = part(1, bf16)[:, 0:CHUNKS], part(1, bf16)[:, CHUNKS:2 * CHUNKS]
        ranks, ranked = part(2)[:, 0:SCOLS], part(3)[:, 0:SCOLS]
        lane_each = part(2, bf16, 2)[:, 0:P * BLOCK].rearrange("p (n c) -> p n c", c=BLOCK)
        slot_each = part(2, bf16, 2)[:, P * BLOCK:(P + BLOCK) * BLOCK].rearrange("p (s c) -> p s c", c=BLOCK)
        moved = part(4, n=VALUES).rearrange("p (b v c) -> p b v c", v=VALUES, c=BLOCK)
        high_f, packed_i, mlow_i, mdst_f, mnorm_f = part(11), part(12, i32), part(13, i32), part(14), part(15)
        dst_g = flat[0:BLOCKS, 13 * CHUNKS:13 * CHUNKS + BLOCK * P].bitcast(i32)
        hot = lane_hot[:, :, :, :].rearrange("p a n c -> p (a n c)")[:, 0:BLOCKS * STAGES * BLOCK].rearrange(
            "p (b q c) -> p b q c", q=STAGES, c=BLOCK)
        PIECE = TILES * P // (2 * ROUNDS)
        residual = [stage[:, b, 0:HALVES * PIECE].rearrange("p (h n) -> p h n", h=HALVES) for b in range(2)]
        stats = sb("stats", [P, 2, BATCH, 6], f32)
        mean_var = sb("mean_var", [P, 2, BATCH, 2], f32)
        std = sb("std", [P, 2, BATCH], f32)
        rstd = sb("rstd", [P, 2, BATCH], f32)
        shift = sb("shift", [P, 2, BATCH], f32)
        out_sb = rows[:, 0:2 * BATCH, :]

        psum = ctx.enter_context(nc.psum_tensor("psum", [P, 8, 2 * F], f32))
        bank = [psum[:, k, :] for k in range(8)]

        def turned_tile(b, t):
            n = b * BATCH + t
            return bank[n // 2][:, n % 2 * F:(n % 2 + 1) * F]

        SUM_BANKS = 4

        w_in = [sem(f"w_in{k}") for k in range(W_RING)]
        x_in = [sem(f"x_in{b}") for b in range(XRING)]
        stored = [sem(f"stored{b}") for b in range(XRING)]
        gathered = [sem(f"gathered{b}") for b in range(RING * GMAX)]
        w_hi_done, w_lo_done = sem("w_hi_done"), sem("w_lo_done")
        x_hi_done, x_lo_done = sem("x_hi_done"), sem("x_lo_done")
        bank_done, evac_done = sem("bank_done"), sem("evac_done")
        edges_in, dst_g_in = sem("edges_in"), sem("dst_g_in")
        residual_in, residual_done = [sem("residual_in0"), sem("residual_in1")], sem("residual_done")
        made, consts, span_done, span_out, ranges_in = sem("made"), sem("consts"), sem("span_done"), sem("span_out"), sem("ranges_in")
        sort_steps = sem("sort_steps")
        hot_done, totals_done, late_done = sem("hot_done"), sem("totals_done"), sem("late_done")
        ranked_done = sem("ranked_done")
        slots_done, lanes_done = sem("slots_done"), sem("lanes_done")
        placed_done, permuted, moved_done, sorted_done = sem("placed_done"), sem("permuted"), sem("moved_done"), sem("sorted_done")
        row_now_done, norm_now_done, off_now_done = sem("row_now_done"), sem("norm_now_done"), sem("off_now_done")
        pool_passed = sem("pool_passed")
        hi_done, lo_done = sem("hi_done"), sem("lo_done")
        dst_rel_done = sem("dst_rel_done")
        onehot_first, onehot_more = sem("onehot_first"), sem("onehot_more")
        sum_first, sum_more = sem("sum_first"), sem("sum_more")
        all_added, acc_done, turned = sem("all_added"), sem("acc_done"), sem("turned")
        stats_done, aggr_done, std_done, rstd_done = sem("stats_done"), sem("aggr_done"), sem("std_done"), sem("rstd_done")
        shift_done, stats_seen = sem("shift_done"), sem("stats_seen")
        norm_act = sem("norm_act")
        out_done = [sem("out_done0"), sem("out_done1")]

        block = ctx.enter_context(nc.Block())

        def col(t, i, n=1):
            return t[:, bass.ds(i, n)]

        def chunk(s, beta, j=0):
            return BLOCKS * SEG_START[s] + SEG[s] * beta + j

        def gather_uses(s, u, it, j):
            per_round = ROUND_GROUPS // RING
            return sum(ROUNDS * per_round for n in SEG[:s] if n > j) + per_round * it + u // RING

        @block.sync
        def _(sp):
            def load_x(part, it, u):
                m, _ = step(part, it, u)
                b = slot(part, u)
                tile = m % TILES if isinstance(m, int) else m - PARTS[part][0] * TILES
                sp.dma_start(x_raw[:, b], xc[:, :, bass.ds(tile * P, P)]).then_inc(x_in[b], 16)

            def next_use(part, it, u):
                distance = XRING
                if part == 0 and u + XRING >= PARTS[0][2]:
                    distance = PARTS[0][2] - u + u % XRING
                return advance(part, it, u, distance)

            def run(part, it, weights=PAIRS):
                for u in range(PARTS[part][2]):
                    m, _ = step(part, it, u)
                    after(sp, x_lo_done, m + 1)
                    use = next_use(part, it, u)
                    if use is not None:
                        load_x(*use)
                    after(sp, evac_done, STAGE_PAIRS * (m + 1))
                    sp.dma_start(table_tiles[bass.ds(m, 1)].rearrange("a p n -> (a p) n"),
                                 stage[:, slot(part, u)]).then_inc(stored[slot(part, u)], 16)
                    if weights + u < PAIRS:
                        load_weight(weights + u)

            def run_part(part):
                rounds = PARTS[part][1]
                if rounds > 1:
                    with sp.Fori(0, rounds - 1) as it:
                        run(part, it)
                run(part, rounds - 1)

            def load_weight(k):
                after(sp, w_lo_done, k - W_RING + 1)
                sp.dma_start(w_raw[:, k % W_RING], weight[k]).then_inc(w_in[k % W_RING], 16)

            load_x(0, 0, 0)
            for k in range(W_RING):
                load_weight(k)
                if k > 0:
                    load_x(0, 0, k)
            run(0, 0, W_RING)
            run(0, 1)
            sp.wait_ge(span_done, 4)
            sp.dma_start(first_dram[:, :], span[:, 0:1]).then_inc(span_out, 16)
            sp.dma_start(further_dram[:, :], further_col[:, :]).then_inc(span_out, 16)
            sp.wait_ge(span_out, 32)
            sp.dma_start(first_all[:, :], first_dram.rearrange("g a -> a g").to_broadcast([P, BLOCKS])).then_inc(ranges_in, 16)
            for s in range(STAGES):
                sp.dma_start(first[:, s * BLOCKS:(s + 1) * BLOCKS], first_dram.rearrange("g a -> a g")).then_inc(ranges_in, 16)
                sp.dma_start(further[:, s * BLOCKS:(s + 1) * BLOCKS], further_dram.rearrange("g a -> a g")).then_inc(ranges_in, 16)
            run(0, 2)
            run_part(1)
            for part in range(LEAD, len(PARTS) - 1):
                run_part(part)

            def load_residual(i, b):
                after(sp, residual_done, i - 1)
                sp.dma_start(residual[b], xc[:, :, bass.ds(i * PIECE, PIECE)]).then_inc(residual_in[b], 16)

            for b in range(XRING):
                sp.wait_ge(stored[b], 16 * STAGE_END_USES[STAGES - 1][b])
            load_residual(0, 0)
            load_residual(1, 1)
            with sp.Fori(1, ROUNDS) as it:
                load_residual(2 * it, 0)
                load_residual(2 * it + 1, 1)

            def store_out(q, b):
                sp.wait_ge(norm_act, BATCH * (q + 1))
                sp.dma_start(out[q * BATCH * P:(q + 1) * BATCH * P, :].rearrange("(t p) f -> p t f", p=P),
                             out_sb[:, b * BATCH:(b + 1) * BATCH, :]).then_inc(out_done[b], 16)

            for q in range(BATCHES):
                store_out(q, q % 2)
            sp.wait_ge(norm_act, BATCH * BATCHES + 1)
            sp.dma_start(out[(TILES - 1) * P:NODES, :], out_sb[0:LAST, 0, :]).then_inc(out_done[0], 16)
            sp.wait_ge(out_done[0], 16 * (BATCHES // 2 + 1))
            sp.wait_ge(out_done[1], 16 * (BATCHES // 2))

        @block.gpsimd
        def _(pool):
            pool.memset(ones_b[:, :], 1.0).then_inc(made, 1)
            pool.memset(later_b[:, :], -1.0).then_inc(made, 1)
            pool.memset(ident[:, :], 0.0).then_inc(made, 1)
            pool.wait_ge(made, 3)
            pool.affine_select(out=later_b[:, :], in_=later_b[:, :], compare_op=ALU.is_ge, fill=0.0, base=0,
                               pattern=[[-1, P]], channel_multiplier=1).then_inc(consts, 1)
            pool.affine_select(out=ident[:, :], in_=ident[:, :], compare_op=ALU.not_equal, fill=1.0, base=0,
                               pattern=[[-1, P]], channel_multiplier=1).then_inc(consts, 1)
            for s in range(STAGES):
                pool.memset(need[:, s:s + 1], float(SEG_START[s + 1] * P if s + 1 < STAGES else 0)).then_inc(consts, 1)
            pool.iota(slot_b[:, :], pattern=[[1, BLOCK]], base=0, channel_multiplier=0,
                      allow_small_or_imprecise_dtypes=True).then_inc(consts, 1)
            pool.iota(lane_b[:, :], pattern=[[1, P]], base=0, channel_multiplier=0,
                      allow_small_or_imprecise_dtypes=True).then_inc(consts, 1)
            pool.iota(lane[:, :], pattern=[[1, P]], base=0, channel_multiplier=0,
                      allow_small_or_imprecise_dtypes=True).then_inc(consts, 1)
            pool.iota(window_base[:, :], pattern=[[P, TILES]], base=0, channel_multiplier=0,
                      allow_small_or_imprecise_dtypes=True).then_inc(consts, 1)
            pool.memset(eps[:, :], EPS).then_inc(consts, 1)
            pool.memset(row_s[:, CHUNKS:], 0).then_inc(consts, 1)
            pool.memset(norm_s[:, CHUNKS:], 0.0).then_inc(consts, 1)
            pool.memset(off_s[:, CHUNKS:], 0.0).then_inc(consts, 1)

            def split_rest(m, b):
                pool.wait_ge(x_hi_done, m + 1)
                pool.tensor_tensor(x_split[:, b, 1], x_raw[:, b], x_split[:, b, 0].bitcast(f32),
                                   ALU.subtract).then_inc(x_lo_done, 1)

            split_rest(0, 0)
            for part in range(LEAD + 1):
                def run(it):
                    for u in range(PARTS[part][2]):
                        m, _ = step(part, it, u)
                        split_rest(m + 1, slot_next(part, u))

                if part == 1:
                    with pool.Fori(0, PARTS[1][1]) as it:
                        run(it)
                else:
                    for it in range(PARTS[part][1]):
                        run(it)

            def wait_tables(s):
                for b in range(XRING):
                    pool.wait_ge(stored[b], 16 * STAGE_END_USES[s][b])

            def gather(s, it, u, stages):
                beta = ROUND_GROUPS * it + u
                after(pool, lo_done, BLOCKS * s + beta - RING + 1)
                pool.wait_ge(row_now_done, BLOCKS * s + beta + 1)
                pool.sem_inc(pool_passed, 1)
                for j in range(SEG[s]):
                    k = (u % RING) * GMAX + j
                    pool.indirect_dma_start(
                        out=rows[:, k, :], out_offset=None, in_=table[0:stages * STAGE_ROWS, :],
                        in_offset=bass.IndirectOffsetOnAxis(ap=row_now[:, u * GMAX + j:u * GMAX + j + 1], axis=0),
                    ).then_inc(gathered[k], 16)

            pool.wait_ge(late_done, 1)
            is_late = pool.value_load(late[0:1, 0:1], min_val=0, max_val=1)

            def segment(s, stages):
                wait_tables(stages - 1)
                if s == 0:
                    for u in range(ROUND_GROUPS):
                        gather(s, 0, u, stages)
                with pool.Fori(1 if s == 0 else 0, ROUNDS) as it:
                    for u in range(ROUND_GROUPS):
                        gather(s, it, u, stages)

            with pool.If(is_late > 0):
                for s in range(STAGES - 1):
                    segment(s, STAGES)
            with pool.If(is_late < 1):
                for s in range(STAGES - 1):
                    segment(s, s + 1)
            segment(STAGES - 1, STAGES)

        @block.scalar
        def _(act):
            for dst_t, src_t in ((rel_i, rel_lanes), (src_i, src_lanes), (dst_i, dst_lanes), (norm_f, norm_lanes)):
                act.dma_start(dst_t, src_t[:, :]).then_inc(edges_in, 16)
            act.dma_start(dst_g, dst_blocks[:, :]).then_inc(dst_g_in, 16)

            def split_leading(m, b, used):
                act.wait_ge(x_in[b], 16 * (used + 1))
                after(act, bank_done, STAGE_PAIRS * (m - 2))
                nc.scalar.activation(x_split[:, b, 0], x_raw[:, b], ACT.Copy).then_inc(x_hi_done, 1)

            def transform(part, it, u):
                m, used = step(part, it, u)
                if PARTS[part][1] == 1 and u + 1 == PARTS[part][2]:
                    m_next, used_next = step(part + 1, 0, 0)
                elif u + 1 < PARTS[part][2]:
                    m_next, used_next = step(part, it, u + 1)
                else:
                    m_next, used_next = step(part, it + 1, 0)
                split_leading(m_next, slot_next(part, u), used_next)
                b = slot(part, u)
                after(act, stored[b], 16 * used)
                for k in range(STAGE_PAIRS):
                    act.wait_ge(bank_done, STAGE_PAIRS * m + k + 1)
                    nc.scalar.activation(stage[:, b, k * 2 * F:(k + 1) * 2 * F],
                                         bank[(b % 2) * STAGE_PAIRS + k], ACT.Copy).then_inc(evac_done, 1)

            def split_weight(k):
                act.wait_ge(w_in[k % W_RING], 16 * (k // W_RING + 1))
                nc.scalar.activation(w_split[:, 0, k].rearrange("p h n -> p (h n)"), w_raw[:, k % W_RING],
                                     ACT.Copy).then_inc(w_hi_done, 1)

            split_leading(0, 0, 0)
            for k in range(STAGE_PAIRS):
                split_weight(k)
            for it in range(PARTS[0][1]):
                for u in range(PARTS[0][2]):
                    if it == 0 and STAGE_PAIRS + u < PAIRS:
                        split_weight(STAGE_PAIRS + u)
                    transform(0, it, u)

            def keep_moved(q, b):
                act.wait_ge(permuted, BATCH_BLOCKS * (q + 1))
                nc.scalar.activation(moved[:, bass.ds(q * BATCH_BLOCKS, BATCH_BLOCKS)].rearrange("p b v c -> p (b v c)"),
                                     bank[SUM_BANKS + b][:, 0:BATCH_BLOCKS * VCOLS], ACT.Copy).then_inc(moved_done, 1)

            with act.Fori(0, 7) as it:
                for half in range(2):
                    transform(1, it, 2 * half)
                    transform(1, it, 2 * half + 1)
                    keep_moved(2 * it + half, half)

            def name_rows(c, r):
                act.copy(row_now[:, r * GMAX:(r + 1) * GMAX], col(row_s, c, GMAX)).then_inc(row_now_done, 1)
                act.copy(norm_now[:, r * GMAX:(r + 1) * GMAX], col(norm_s, c, GMAX)).then_inc(norm_now_done, 1)
                act.copy(off_now[:, r * GMAX:(r + 1) * GMAX], col(off_s, c, GMAX)).then_inc(off_now_done, 1)

            def scale(s, it, u):
                beta = ROUND_GROUPS * it + u
                g = BLOCKS * s + beta
                act.wait_ge(norm_now_done, g + 1)
                act.wait_ge(onehot_first, g + 1)
                for j in range(SEG[s]):
                    k = (u % RING) * GMAX + j
                    act.wait_ge(gathered[k], 16 * (gather_uses(s, u, it, j) + 1))
                    nc.scalar.activation(msg[:, u % 2, 0, j, :], rows[:, k, :], ACT.Copy,
                                         scale=norm_now[:, u * GMAX + j:u * GMAX + j + 1]).then_inc(hi_done, 1)
                if isinstance(beta, int) and beta + RING >= BLOCKS and s + 1 < STAGES:
                    c = chunk(s + 1, beta + RING - BLOCKS)
                else:
                    c = chunk(s, beta + RING)
                name_rows(c, (u + RING) % NAMED)

            for u in range(PARTS[LEAD][2]):
                if u == 6:
                    act.wait_ge(sorted_done, 1)
                    for g in range(RING):
                        name_rows(chunk(0, g), g)
                transform(LEAD, 0, u)
            act.wait_ge(late_done, 1)
            is_late = act.value_load(late[0:1, 0:1], min_val=0, max_val=1)

            def segment(s, beside):
                def run(it):
                    steps = beside_groups(s, it) if beside else []
                    for u in range(ROUND_GROUPS):
                        scale(s, it, u)
                        if u < len(steps):
                            transform(*steps[u])

                if s == 0:
                    run(0)
                with act.Fori(1 if s == 0 else 0, ROUNDS - 2) as it:
                    run(it)
                run(ROUNDS - 2)
                run(ROUNDS - 1)

            with act.If(is_late > 0):
                for part in range(LEAD + 1, len(PARTS) - 1):
                    if PARTS[part][1] > 1:
                        with act.Fori(0, PARTS[part][1]) as it:
                            for u in range(PARTS[part][2]):
                                transform(part, it, u)
                    else:
                        for u in range(PARTS[part][2]):
                            transform(part, 0, u)
                for s in range(STAGES - 1):
                    segment(s, False)
            with act.If(is_late < 1):
                for s in range(STAGES - 1):
                    segment(s, True)
            segment(STAGES - 1, False)

            def normalise(q, b, uses, tiles):
                act.wait_ge(aggr_done, q * BATCH + tiles)
                nc.scalar.activation(std[:, b, 0:tiles], mean_var[:, b, 0:tiles, 1], ACT.Sqrt,
                                     bias=eps[:, 0:1]).then_inc(std_done, 1)
                if uses is not None:
                    act.wait_ge(out_done[b], 16 * uses)
                act.wait_ge(shift_done, q + 1)
                for t in range(tiles):
                    nc.scalar.activation(out_sb[:, b * BATCH + t, :], turned_tile(b, t), ACT.Identity,
                                         bias=shift[:, b, t:t + 1], scale=rstd[:, b, t:t + 1]).then_inc(norm_act, 1)

            normalise(0, 0, None, BATCH)
            normalise(1, 1, None, BATCH)
            with act.Fori(1, BATCHES // 2) as i:
                normalise(2 * i, 0, i, BATCH)
                normalise(2 * i + 1, 1, i, BATCH)
            normalise(BATCHES, 0, BATCHES // 2, 1)

        @block.vector
        def _(dve):
            chain = [0]

            def link(instruction):
                chain[0] += 1
                instruction.then_inc(sort_steps, 1)
                dve.wait_ge(sort_steps, chain[0])

            def next_rest(part, it, u):
                m, _ = step(part, it, u)
                b = slot_next(part, u)
                dve.wait_ge(x_hi_done, m + 2)
                nc.vector.tensor_tensor(x_split[:, b, 1], x_raw[:, b], x_split[:, b, 0].bitcast(f32),
                                        ALU.subtract).then_inc(x_lo_done, 1)

            def split_weight(k):
                dve.wait_ge(w_hi_done, k + 1)
                nc.vector.tensor_tensor(w_split[:, 1, k].rearrange("p h n -> p (h n)"), w_raw[:, k % W_RING],
                                        w_split[:, 0, k].rearrange("p h n -> p (h n)").bitcast(f32),
                                        ALU.subtract).then_inc(w_lo_done, 1)

            def blocks(t):
                return t.rearrange("p (b c) -> p b c", c=BLOCK)

            V = nc.vector
            for k in range(STAGE_PAIRS):
                split_weight(k)
            dve.wait_ge(edges_in, 16 * 4)
            V.tensor_single_scalar(low_i, rel_i, STAGE_RELS - 1, ALU.bitwise_and)
            link(V.tensor_single_scalar(key_i, rel_i, REL_BITS, ALU.arith_shift_right))
            for q in range(STAGES):
                V.tensor_single_scalar(hot[:, :, q, :], blocks(key_i), float(q), ALU.is_equal).then_inc(hot_done, 1)
            split_weight(STAGE_PAIRS)
            V.tensor_single_scalar(dlow_i, dst_i, P - 1, ALU.bitwise_and)
            V.tensor_single_scalar(dhi_i, dst_i, P.bit_length() - 1, ALU.arith_shift_right)
            link(V.scalar_tensor_tensor(out=srow_i, in0=src_i, scalar=float(STAGE_RELS), in1=low_i,
                                        op0=ALU.mult, op1=ALU.add))
            link(V.scalar_tensor_tensor(out=row_i, in0=key_i, scalar=float(STAGE_ROWS), in1=srow_i,
                                        op0=ALU.mult, op1=ALU.add))
            link(V.scalar_tensor_tensor(out=pack_i, in0=row_i, scalar=float(P), in1=dlow_i,
                                        op0=ALU.mult, op1=ALU.add))
            split_weight(STAGE_PAIRS + 1)

            dve.wait_ge(dst_g_in, 16)
            V.tensor_reduce(span[:, 0:1], dst_g, AX.X, ALU.min).then_inc(span_done, 1)
            V.tensor_reduce(span[:, 1:2], dst_g, AX.X, ALU.max).then_inc(span_done, 1)
            split_weight(STAGE_PAIRS + 2)
            dve.wait_ge(span_done, 2)
            V.tensor_tensor(span[:, 2:3], span[:, 1:2], span[:, 0:1], ALU.subtract).then_inc(span_done, 1)
            dve.wait_ge(span_done, 3)
            V.tensor_single_scalar(further_col[:, :], span[:, 2:3], P.bit_length() - 1,
                                   ALU.arith_shift_right).then_inc(span_done, 1)

            V.tensor_single_scalar(digit_i[0], pack_i, 255, ALU.bitwise_and)
            V.tensor_scalar(digit_i[1], pack_i, 8, 255, ALU.arith_shift_right, ALU.bitwise_and)
            link(V.tensor_single_scalar(digit_i[2], pack_i, 16, ALU.arith_shift_right))
            for k in range(STAGE_PAIRS + 3, PAIRS):
                split_weight(k)
            dve.wait_ge(w_lo_done, PAIRS)
            dve.wait_ge(consts, CONSTS)
            link(V.memset(goes_on, 1.0))
            link(V.memset(goes_on.rearrange("p (b n) -> p b n", n=STAGES * BLOCK)[:, :, 0:1], 0.0))
            for v, source in enumerate((*digit_i, dhi_i)):
                V.tensor_copy(val[:, :, v], blocks(source))
            link(V.tensor_copy(val[:, :, 4], blocks(norm_f)))
            link(V.tensor_tensor(blocks(rest1), blocks(norm_f), val[:, :, 4], ALU.subtract))
            link(V.tensor_copy(val[:, :, 5], blocks(rest1)))
            link(V.tensor_tensor(blocks(rest2), blocks(rest1), val[:, :, 5], ALU.subtract))
            link(V.tensor_copy(val[:, :, 6], blocks(rest2)))

            for i in range(BLOCKS // SLICE):
                b = SUM_BANKS + 2 * (i % 2)
                dve.wait_ge(totals_done, i + 1)
                link(V.tensor_tensor_scan(ranks, goes_on[:, :], bank[b][:, 0:SCOLS], 0.0, ALU.mult, ALU.add))
                V.tensor_copy(cum[:, i * SLICE:(i + 1) * SLICE, :],
                              ranks.rearrange("p (b q c) -> p b q c", q=STAGES, c=BLOCK)[:, :, :, BLOCK - 1])
                link(V.tensor_tensor(ranked, ranks, bank[b + 1][:, 0:SCOLS], ALU.add))
                link(V.tensor_tensor(ranks, ranked, hot[:, i * SLICE:(i + 1) * SLICE].rearrange("p b q c -> p (b q c)"),
                                     ALU.mult))
                link(V.tensor_reduce(pos_f[:, i * SLICE * BLOCK:(i + 1) * SLICE * BLOCK].rearrange("p (b c) -> p b c", c=BLOCK),
                                     ranks.rearrange("p (b q c) -> p b c q", q=STAGES, c=BLOCK), AX.X, ALU.add))
                dve.sem_inc(ranked_done, 1)
            link(V.tensor_reduce(least[:, :], cum[:, :, :].rearrange("p b q -> p q b"), AX.X, ALU.min))
            link(V.tensor_tensor(short[:, :], least[:, :], need[:, :], ALU.is_lt))
            V.tensor_reduce(late[:, :], short[:, :], AX.X, ALU.max).then_inc(late_done, 1)
            link(V.tensor_copy(pos_i, pos_f))
            link(V.tensor_single_scalar(plane_i, pos_i, P - 1, ALU.bitwise_and))
            link(V.tensor_single_scalar(pslot_i, pos_i, P.bit_length() - 1, ALU.arith_shift_right))
            V.tensor_copy(lane_each, lane_b[:, :].rearrange("p (n a) -> p n a", a=1).to_broadcast([P, P, BLOCK]))
            V.tensor_copy(slot_each, slot_b[:, :].rearrange("p (n a) -> p n a", a=1).to_broadcast([P, BLOCK, BLOCK]))
            link(V.tensor_copy(plane_b, plane_i))
            link(V.tensor_copy(pslot_b, pslot_i))

            def place_batch(q):
                after(dve, placed_done, BATCH_BLOCKS * q)
                V.tensor_tensor(slot_hot, col(pslot_b, q * BATCH_BLOCKS * BLOCK, BATCH_BLOCKS * BLOCK).rearrange(
                                    "p (e a c) -> p e a c", a=1, c=BLOCK).to_broadcast([P, BATCH_BLOCKS, BLOCK, BLOCK]),
                                slot_each.rearrange("p (a s) c -> p a s c", a=1).to_broadcast(
                                    [P, BATCH_BLOCKS, BLOCK, BLOCK]),
                                ALU.is_equal).then_inc(slots_done, 1)
                for e in range(BATCH_BLOCKS):
                    n = BATCH_BLOCKS * q + e
                    after(dve, permuted, n - 1)
                    V.tensor_tensor(lane_hot[:, e % 2], col(plane_b, n * BLOCK, BLOCK).rearrange(
                                        "p (a c) -> p a c", a=1).to_broadcast([P, P, BLOCK]),
                                    lane_each, ALU.is_equal).then_inc(lanes_done, 1)
                    dve.wait_ge(slots_done, q + 1)
                    V.tensor_tensor(placed[:, e % 2],
                                    slot_hot[:, e:e + 1].to_broadcast([P, VALUES, BLOCK, BLOCK]),
                                    val[:, bass.ds(n, 1)].rearrange("p b v c -> p (b v) c").rearrange(
                                        "p v (a c) -> p v a c", a=1).to_broadcast([P, VALUES, BLOCK, BLOCK]),
                                    ALU.mult).then_inc(placed_done, 1)

            place_batch(0)
            with dve.Fori(1, SORT_BATCHES) as q:
                place_batch(q)

            dve.wait_ge(moved_done, SORT_BATCHES)
            dve.wait_ge(ranges_in, 16 * (1 + 2 * STAGES))

            def unpack(s):
                def seg(t):
                    return t.rearrange("p (b c) -> p b c", c=BLOCK)[:, :, SEG_START[s]:SEG_START[s + 1]]

                def summing(t):
                    return t[:, BLOCKS * SEG_START[s]:BLOCKS * SEG_START[s + 1]].rearrange("p (b c) -> p b c", c=SEG[s])

                part_of = [moved[:, :, v, SEG_START[s]:SEG_START[s + 1]] for v in range(VALUES)]
                V.tensor_tensor(seg(mnorm_f), part_of[4], part_of[5], ALU.add)
                link(V.scalar_tensor_tensor(out=seg(high_f), in0=part_of[2], scalar=256.0, in1=part_of[1],
                                            op0=ALU.mult, op1=ALU.add))
                V.tensor_tensor(summing(norm_s), seg(mnorm_f), part_of[6], ALU.add)
                link(V.scalar_tensor_tensor(out=seg(packed_i), in0=seg(high_f), scalar=256.0, in1=part_of[0],
                                            op0=ALU.mult, op1=ALU.add))
                V.tensor_single_scalar(summing(row_s), seg(packed_i), P.bit_length() - 1, ALU.arith_shift_right)
                link(V.tensor_single_scalar(seg(mlow_i), seg(packed_i), P - 1, ALU.bitwise_and))
                link(V.scalar_tensor_tensor(out=seg(mdst_f), in0=part_of[3], scalar=float(P), in1=seg(mlow_i),
                                            op0=ALU.mult, op1=ALU.add))
                link(V.tensor_tensor(summing(off_s), seg(mdst_f),
                                     first_all[:, :].rearrange("p (g a) -> p g a", a=1).to_broadcast([P, BLOCKS, SEG[s]]),
                                     ALU.subtract))

            unpack(0)
            dve.sem_inc(sorted_done, 1)
            for s in range(1, STAGES):
                unpack(s)
            dve.sem_inc(sorted_done, 1)
            link(V.memset(acc[:, :, :], 0.0))

            more = dve.alloc_register("dve_more")
            dve.reg_mov(more, 0)

            def lane_is(offsets, b, n, opened):
                V.tensor_tensor(onehot[:, b, 0:n, :],
                                lane[:, :].rearrange("p (a n) -> p a n", a=1).to_broadcast([P, n, P]),
                                offsets.rearrange("p (g a) -> p g a", a=1).to_broadcast([P, n, P]),
                                ALU.is_equal).then_inc(opened, 1)

            def add_window(node, b):
                place = acc[:, :, bass.ds(node, P)]
                V.tensor_tensor(place, place, psum[:, SUM_BANKS + HALVES * b:SUM_BANKS + HALVES * (b + 1), 0:P],
                                ALU.add).then_inc(acc_done, 1)

            def open_group(g, slot, n):
                dve.wait_ge(off_now_done, g + 1)
                lane_is(off_now[:, slot * GMAX:slot * GMAX + n], slot % 2, n, onehot_first)

            def split_group(s, it, u):
                beta = ROUND_GROUPS * it + u
                for j in range(SEG[s]):
                    dve.wait_ge(hi_done, chunk(s, beta, j + 1))
                    k = (u % RING) * GMAX + j
                    split = V.scalar_tensor_tensor(out=msg[:, u % 2, 1, j, :], in0=rows[:, k, :],
                                                   scalar=norm_now[:, u * GMAX + j:u * GMAX + j + 1],
                                                   in1=msg[:, u % 2, 0, j, :].bitcast(f32),
                                                   op0=ALU.mult, op1=ALU.subtract)
                split.then_inc(lo_done, 1)

            def find_group(g):
                node = dve.value_load(first[0:1, bass.ds(g, 1)], min_val=0, max_val=NODES - 1)
                windows = dve.value_load(further[0:1, bass.ds(g, 1)], min_val=0, max_val=TILES - 1)
                return node, windows, dve.snap(more) + g

            def finish_group(g, slot, node, windows, added):
                b = slot % 2
                dve.wait_ge(sum_first, g + 1)
                if not isinstance(g, int) or g > 0:
                    dve.wait_ge(acc_done, added)
                add_window(node, b)
                with dve.If(windows > 0):
                    with dve.Fori(1, windows + 1) as w:
                        V.tensor_scalar(dst_rel[:, :], off_now[:, slot * GMAX:(slot + 1) * GMAX], col(window_base, w),
                                        None, ALU.subtract).then_inc(dst_rel_done, 1)
                        dve.reg_add(more, more, 1)
                        count = dve.snap(more)
                        dve.wait_ge(dst_rel_done, count)
                        lane_is(dst_rel[:, :], b, GMAX, onehot_more)
                        dve.wait_ge(sum_more, count)
                        dve.wait_ge(acc_done, count + g)
                        add_window(nc.s_assert_within(node + w * P, 0, NODES - 1), b)

            def add_residual(it, b, u):
                g = BLOCKS * (STAGES - 1) + ROUND_GROUPS * it + u
                added = dve.snap(more) + g
                dve.wait_ge(residual_in[b], 16 * (it + 1))
                dve.wait_ge(acc_done, added)
                place = acc[:, :, bass.ds((2 * it + b) * PIECE, PIECE)]
                V.tensor_tensor(place, place, residual[b], ALU.add).then_inc(residual_done, 1)
                dve.wait_ge(residual_done, 2 * it + b + 1)

            def group(s, it, u):
                g = BLOCKS * s + ROUND_GROUPS * it + u
                begins = isinstance(g, int) and g == 0
                if not begins:
                    place = find_group(g - 1)
                split_group(s, it, u)
                if not begins:
                    finish_group(g - 1, (u - 1) % NAMED, *place)
                n = max(SEG[s], SEG[min(s + 1, STAGES - 1)]) if u == ROUND_GROUPS - 1 else SEG[s]
                open_group(g + 1, (u + 1) % NAMED, n)

            dve.wait_ge(x_lo_done, step(LEAD + 1, 0, 0)[0] + 1)
            is_late = dve.value_load(late[0:1, 0:1], min_val=0, max_val=1)
            open_group(0, 0, SEG[0])

            def segment(s, beside):
                def run(it):
                    steps = beside_groups(s, it) if beside else []
                    for u in range(ROUND_GROUPS):
                        group(s, it, u)
                        if u < len(steps):
                            next_rest(*steps[u])
                        if s == STAGES - 1 and u in (3, 7):
                            add_residual(it, u // 4, u)

                if s == 0:
                    run(0)
                with dve.Fori(1 if s == 0 else 0, ROUNDS - 2) as it:
                    run(it)
                run(ROUNDS - 2)
                run(ROUNDS - 1)

            with dve.If(is_late > 0):
                for part in range(LEAD + 1, len(PARTS) - 1):
                    if PARTS[part][1] > 1:
                        with dve.Fori(0, PARTS[part][1]) as it:
                            for u in range(PARTS[part][2]):
                                next_rest(part, it, u)
                    else:
                        for u in range(PARTS[part][2]):
                            next_rest(part, 0, u)
                for s in range(STAGES - 1):
                    segment(s, False)
            with dve.If(is_late < 1):
                for s in range(STAGES - 1):
                    segment(s, True)
            segment(STAGES - 1, False)
            finish_group(GROUPS - 1, NAMED - 1, *find_group(GROUPS - 1))
            dve.wait_ge(acc_done, dve.snap(more) + GROUPS)
            dve.sem_inc(all_added, 1)

            def take_stats(q, b, tiles):
                for t in range(tiles):
                    if t % 2 == 0:
                        dve.wait_ge(turned, q * BATCH + min(t + 2, tiles))
                    nc.vector.bn_stats(stats[:, b, t, :], turned_tile(b, t)).then_inc(stats_done, 1)
                dve.wait_ge(stats_done, q * BATCH + tiles)
                dve.sem_inc(stats_seen, 1)
                for t in range(tiles):
                    nc.vector.bn_aggr(mean_var[:, b, t, :], stats[:, b, t, :]).then_inc(aggr_done, 1)
                dve.wait_ge(std_done, q + 1)
                nc.vector.reciprocal(rstd[:, b, 0:tiles], std[:, b, 0:tiles]).then_inc(rstd_done, 1)
                dve.wait_ge(rstd_done, q + 1)
                nc.vector.scalar_tensor_tensor(out=shift[:, b, 0:tiles], in0=mean_var[:, b, 0:tiles, 0], scalar=-1.0,
                                               in1=rstd[:, b, 0:tiles], op0=ALU.mult, op1=ALU.mult).then_inc(shift_done, 1)

            take_stats(0, 0, BATCH)
            take_stats(1, 1, BATCH)
            with dve.Fori(1, BATCHES // 2) as i:
                take_stats(2 * i, 0, BATCH)
                take_stats(2 * i + 1, 1, BATCH)
            take_stats(BATCHES, 0, 1)

        @block.tensor
        def _(pe):
            PRODUCTS = ((0, 0), (0, 1), (1, 0))

            def transform(part, it, u):
                s, b = PARTS[part][0], slot(part, u)
                m, _ = step(part, it, u)
                pe.wait_ge(x_lo_done, m + 1)
                back = 1 if u == 0 and part <= 1 and isinstance(it, int) else 2
                for k in range(STAGE_PAIRS):
                    pair = STAGE_PAIRS * s + k
                    if part == 0 and it == 0 or (u == 0 and k == 0):
                        pe.wait_ge(w_lo_done, pair + 1)
                    after(pe, evac_done, STAGE_PAIRS * (m - back) + k + 1)
                    steps = [(a, c, h) for a, c in PRODUCTS for h in range(HALVES)]
                    for n, (a, c, h) in enumerate(steps):
                        last = nc.tensor.matmul(bank[(b % 2) * STAGE_PAIRS + k], x_split[:, b, a, h],
                                                w_split[:, c, pair, h], start=n == 0, stop=n == len(steps) - 1)
                    last.then_inc(bank_done, 1)

            BEFORE_RANKS = 10
            opening = [(0, it, u) for it in range(PARTS[0][1]) for u in range(PARTS[0][2])]
            for at in opening[:BEFORE_RANKS]:
                transform(*at)
            pe.wait_ge(hot_done, STAGES)
            for i in range(BLOCKS // SLICE):
                b = SUM_BANKS + 2 * (i % 2)
                after(pe, ranked_done, i - 1)
                slice_hot = hot[:, i * SLICE:(i + 1) * SLICE].rearrange("p b q c -> p (b q c)")
                nc.tensor.matmul(bank[b][:, 0:SCOLS], ones_b[:, :], slice_hot, start=True, stop=True)
                nc.tensor.matmul(bank[b + 1][:, 0:SCOLS], later_b[:, :], slice_hot,
                                 start=True, stop=True).then_inc(totals_done, 1)
                transform(*opening[BEFORE_RANKS + i])
            for at in opening[BEFORE_RANKS + BLOCKS // SLICE:]:
                transform(*at)

            def permute(q, b, which):
                if which[0] == 0:
                    after(pe, moved_done, q - 1)
                for e in which:
                    pe.wait_ge(placed_done, BATCH_BLOCKS * q + e + 1)
                    for c in range(BLOCK):
                        last = nc.tensor.matmul(bank[SUM_BANKS + b][:, e * VCOLS:(e + 1) * VCOLS],
                                                lane_hot[:, e % 2, :, c],
                                                placed[:, e % 2, :, :, c].rearrange("p v s -> p (v s)"),
                                                start=c == 0, stop=c == BLOCK - 1, skip_group_check=True)
                    last.then_inc(permuted, 1)

            def sort_round(it):
                for half in range(2):
                    permute(2 * it + half, half, (0, 1))
                    transform(1, it, 2 * half)
                    permute(2 * it + half, half, (2, 3))
                    transform(1, it, 2 * half + 1)

            sort_round(0)
            with pe.Fori(1, PARTS[1][1]) as it:
                sort_round(it)
            for u in range(PARTS[LEAD][2]):
                transform(LEAD, 0, u)

            more = pe.alloc_register("pe_more")
            pe.reg_mov(more, 0)

            def sum_group(b, n, done):
                for j in range(n):
                    for h in range(HALVES):
                        for a in range(2):
                            last = nc.tensor.matmul(psum[:, SUM_BANKS + HALVES * b + h, 0:P],
                                                    msg[:, b, a, j, h * P:(h + 1) * P],
                                                    onehot[:, b, j, :], start=j == 0 and a == 0,
                                                    stop=j == n - 1 and a == 1)
                last.then_inc(done, 1)

            def group(s, it, u):
                g = BLOCKS * s + ROUND_GROUPS * it + u
                windows = pe.value_load(further[0:1, bass.ds(g, 1)], min_val=0, max_val=TILES - 1)
                pe.wait_ge(lo_done, g + 1)
                sum_group(u % 2, SEG[s], sum_first)
                with pe.If(windows > 0):
                    with pe.Fori(1, windows + 1):
                        pe.reg_add(more, more, 1)
                        pe.wait_ge(onehot_more, pe.snap(more))
                        sum_group(u % 2, SEG[s], sum_more)

            pe.wait_ge(moved_done, SORT_BATCHES)
            pe.wait_ge(ranges_in, 16 * (1 + 2 * STAGES))
            pe.wait_ge(late_done, 1)
            is_late = pe.value_load(late[0:1, 0:1], min_val=0, max_val=1)

            def segment(s, beside):
                def run(it):
                    steps = beside_groups(s, it) if beside else []
                    for u in range(ROUND_GROUPS):
                        if u < len(steps):
                            transform(*steps[u])
                        group(s, it, u)

                with pe.Fori(0, ROUNDS - 2) as it:
                    run(it)
                run(ROUNDS - 2)
                run(ROUNDS - 1)

            with pe.If(is_late > 0):
                for part in range(LEAD + 1, len(PARTS) - 1):
                    if PARTS[part][1] > 1:
                        with pe.Fori(0, PARTS[part][1]) as it:
                            for u in range(PARTS[part][2]):
                                transform(part, it, u)
                    else:
                        for u in range(PARTS[part][2]):
                            transform(part, 0, u)
                for s in range(STAGES - 1):
                    segment(s, False)
            with pe.If(is_late < 1):
                for s in range(STAGES - 1):
                    segment(s, True)
            segment(STAGES - 1, False)

            def turn(q, b, tiles, first):
                for t in range(tiles):
                    if not first and t % 2 == 0:
                        pe.wait_ge(norm_act, BATCH * (q - 2) + t + 2)
                    for h in range(HALVES):
                        last = nc.tensor.transpose(turned_tile(b, t)[:, h * P:(h + 1) * P],
                                                   acc[:, h, bass.ds((q * BATCH + t) * P, P)], ident[:, :])
                    last.then_inc(turned, 1)

            pe.wait_ge(consts, CONSTS)
            pe.wait_ge(all_added, 1)
            for q in range(BATCHES):
                turn(q, q % 2, BATCH, q < 2)
            turn(BATCHES, 0, 1, False)


def kernel(x, src, dst, edge_type_16, edge_weight1, L0_gnn_weight):
    import numpy as np
    import concourse.bacc as bacc
    from concourse.bass_utils import run_bass_kernel_spmd

    x, w = np.asarray(x), np.asarray(L0_gnn_weight)
    nodes, feats = x.shape
    rels = w.shape[0]
    edges = np.asarray(src).shape[0]
    tiles = -(-nodes // P)
    chunks = -(-edges // (P * BLOCK)) * BLOCK
    x_rows = np.concatenate([x, np.zeros((tiles * P - nodes, feats), x.dtype)])

    def padded(a, fill):
        a = np.asarray(a).reshape(-1)
        return np.concatenate([a, np.full(chunks * P - edges, fill, a.dtype)])

    def lanes(a):
        return np.ascontiguousarray(a.reshape(chunks, P).T)

    dst_flat = padded(dst, nodes - 1)
    arrays = {
        "x_cols": np.ascontiguousarray(x_rows.T),
        "weight": np.ascontiguousarray(w.reshape(rels // 2, 2, feats // P, P, feats).transpose(0, 3, 2, 1, 4))
                    .reshape(rels // 2, P, -1),
        "src_lanes": lanes(padded(src, 0)),
        "rel_lanes": lanes(padded(edge_type_16, 0)),
        "dst_lanes": lanes(dst_flat),
        "norm_lanes": lanes(padded(edge_weight1, 0)),
        "dst_blocks": dst_flat.reshape(chunks // BLOCK, BLOCK * P),
    }
    nc = bacc.Bacc("TRN2", target_bir_lowering=False, num_devices=1)
    args = [nc.dram_tensor(n, a.shape, mybir.dt.from_np(a.dtype), kind="ExternalInput").ap()
            for n, a in arrays.items()]
    out = nc.dram_tensor("out", (nodes, feats), mybir.dt.float32, kind="ExternalOutput").ap()
    resnorm_gnn(nc, *args, out)
    result = run_bass_kernel_spmd(nc, [arrays], core_ids=[0])
    return result.results[0]["out"]
```
